# Optimizing a Trainium2 kernel written in Bass

```python
import numpy as np
import jax
import jax.numpy as jnp

def _softmax(x, axis=-1):
    return jax.nn.softmax(x, axis=axis)

def _gelu(x):
    return jax.nn.gelu(x, approximate=True)

def _silu(x):
    return jax.nn.silu(x)

def _sigmoid(x):
    return jax.nn.sigmoid(x)

def _layernorm(x, axis=-1, eps=1e-05):
    m = jnp.mean(x, axis=axis, keepdims=True)
    v = jnp.var(x, axis=axis, keepdims=True)
    return (x - m) / jnp.sqrt(v + eps)

def _scatter_add(tgt, idx, src, axis=0):
    return tgt.at[idx].add(src)

def _segment_sum(src, seg, n):
    return jax.ops.segment_sum(src, seg, n)
kernel_name = 'mk_seq_postln_d2_jaxref_r8_e1020f'

def setup_inputs(seed: int=0):
    np.random.seed(seed)
    _w = jnp.asarray

    def _L0_attn_setup():
        import jax, jax.numpy as jnp
        import numpy as np
        B, N, W = (4, 512, 128)
        H, A, P = (16, 64, 64)
        key = jax.random.key(seed)
        ks = jax.random.split(key, 11)
        u = lambda k, shape: jax.random.uniform(k, shape, jnp.float32, -0.05, 0.05)
        glorot_v = (2.0 / (W + A)) ** 0.5
        return {'x': jax.random.normal(ks[0], (B, N, W), jnp.float32), 'k1': u(ks[1], (H, W)), 'k2': u(ks[2], (H, W)), 'k3': u(ks[3], (H, W)), 'a1': u(ks[4], (H, P, 1)), 'a2': u(ks[5], (H, P, 1)), 'b1': u(ks[6], (H, P, 1)), 'b2': u(ks[7], (H, P, 1)), 'c': u(ks[8], (H, P, 1)), 'value_weight': jax.random.normal(ks[9], (H, W, A), jnp.float32) * glorot_v, 'output_weight': jax.random.normal(ks[10], (H, W, A), jnp.float32) * glorot_v}
    _L0_attn_in = _L0_attn_setup()

    def _L0_ffn_setup():
        import jax, jax.numpy as jnp
        import numpy as np
        B, S, D, H, E = (4, 256, 128, 256, 8)
        key = jax.random.key(seed)
        ks = jax.random.split(key, 8)
        scale = 0.02
        return {'x': jax.random.normal(ks[0], (B, S, D), dtype=jnp.float32), 'Wr': jax.random.normal(ks[1], (D, E), dtype=jnp.float32) * scale, 'br': jnp.zeros((E,), dtype=jnp.float32), 'W1': jax.random.normal(ks[2], (E, D, H), dtype=jnp.float32) * scale, 'b1': jnp.zeros((E, H), dtype=jnp.float32), 'W2': jax.random.normal(ks[3], (E, H, D), dtype=jnp.float32) * scale, 'b2': jnp.zeros((E, D), dtype=jnp.float32)}
    _L0_ffn_in = _L0_ffn_setup()

    def _L1_attn_setup():
        import jax, jax.numpy as jnp
        import numpy as np
        DIM = 128
        HEADS = 16
        HEAD_DIM = DIM // HEADS
        NUM_FILTERS = 4
        NUM_TAPS = 101
        RES = 64

        def _fir_fft(c, sig):
            R = sig.shape[0]
            L = R + c.shape[0] - 1
            out = jnp.fft.ifft(jnp.fft.fft(sig, n=L) * jnp.fft.fft(c, n=L)).real
            return out[:R]
        key = jax.random.key(seed)
        ks = jax.random.split(key, 5)
        B, S = (2, 256)
        x = jax.random.normal(ks[0], (B, S, DIM), dtype=jnp.float32)
        Wqkv = jax.random.normal(ks[1], (3 * DIM, DIM), dtype=jnp.float32) * DIM ** (-0.5)
        Wout = jax.random.normal(ks[2], (DIM, DIM), dtype=jnp.float32) * DIM ** (-0.5)
        Wpos = jax.random.normal(ks[3], (HEADS, NUM_FILTERS), dtype=jnp.float32) * 0.5
        coeffs = jax.random.normal(ks[4], (NUM_FILTERS, NUM_TAPS), dtype=jnp.float32) * 0.05
        return {'x': x, 'Wqkv': Wqkv, 'Wout': Wout, 'Wpos': Wpos, 'coeffs': coeffs}
    _L1_attn_in = _L1_attn_setup()

    def _L1_ffn_setup():
        import jax, jax.numpy as jnp
        import numpy as np
        B, S, H, F, E = (1, 256, 128, 256, 8)

        def _swiglu(x, wg, wu, wd):
            return jax.nn.silu(x @ wg.T) * (x @ wu.T) @ wd.T
        key = jax.random.key(seed)
        ks = jax.random.split(key, 8)
        sc = 1.0 / np.sqrt(H)
        scf = 1.0 / np.sqrt(F)
        return {'hidden_states': jax.random.normal(ks[0], (B, S, H), jnp.float32), 'gate_w': jax.random.normal(ks[1], (E, H), jnp.float32) * sc, 'shared_gate': jax.random.normal(ks[2], (F, H), jnp.float32) * sc, 'shared_up': jax.random.normal(ks[3], (F, H), jnp.float32) * sc, 'shared_down': jax.random.normal(ks[4], (H, F), jnp.float32) * scf, 'r_gate': jax.random.normal(ks[5], (E, F, H), jnp.float32) * sc, 'r_up': jax.random.normal(ks[6], (E, F, H), jnp.float32) * sc, 'r_down': jax.random.normal(ks[7], (E, H, F), jnp.float32) * scf}
    _L1_ffn_in = _L1_ffn_setup()
    _d = {'L0_attn_x': _L0_attn_in['x'], 'L0_attn_k1': _L0_attn_in['k1'], 'L0_attn_k2': _L0_attn_in['k2'], 'L0_attn_k3': _L0_attn_in['k3'], 'L0_attn_a1': _L0_attn_in['a1'], 'L0_attn_a2': _L0_attn_in['a2'], 'L0_attn_b1': _L0_attn_in['b1'], 'L0_attn_b2': _L0_attn_in['b2'], 'L0_attn_c': _L0_attn_in['c'], 'L0_attn_value_weight': _L0_attn_in['value_weight'], 'L0_attn_output_weight': _L0_attn_in['output_weight'], 'L0_ffn_Wr': _L0_ffn_in['Wr'], 'L0_ffn_br': _L0_ffn_in['br'], 'L0_ffn_W1': _L0_ffn_in['W1'], 'L0_ffn_b1': _L0_ffn_in['b1'], 'L0_ffn_W2': _L0_ffn_in['W2'], 'L0_ffn_b2': _L0_ffn_in['b2'], 'L1_attn_Wqkv': _L1_attn_in['Wqkv'], 'L1_attn_Wout': _L1_attn_in['Wout'], 'L1_attn_Wpos': _L1_attn_in['Wpos'], 'L1_attn_coeffs': _L1_attn_in['coeffs'], 'L1_ffn_gate_w': _L1_ffn_in['gate_w'], 'L1_ffn_shared_gate': _L1_ffn_in['shared_gate'], 'L1_ffn_shared_up': _L1_ffn_in['shared_up'], 'L1_ffn_shared_down': _L1_ffn_in['shared_down'], 'L1_ffn_r_gate': _L1_ffn_in['r_gate'], 'L1_ffn_r_up': _L1_ffn_in['r_up'], 'L1_ffn_r_down': _L1_ffn_in['r_down']}
    _x0 = _d['L0_attn_x']
    _d['L0_attn_x'] = jax.random.normal(jax.random.fold_in(jax.random.key(seed), 1), (16, 512, 128), dtype=_x0.dtype)
    del _x0
    return _d

def reference(L0_attn_x, L0_attn_k1, L0_attn_k2, L0_attn_k3, L0_attn_a1, L0_attn_a2, L0_attn_b1, L0_attn_b2, L0_attn_c, L0_attn_value_weight, L0_attn_output_weight, L0_ffn_Wr, L0_ffn_br, L0_ffn_W1, L0_ffn_b1, L0_ffn_W2, L0_ffn_b2, L1_attn_Wqkv, L1_attn_Wout, L1_attn_Wpos, L1_attn_coeffs, L1_ffn_gate_w, L1_ffn_shared_gate, L1_ffn_shared_up, L1_ffn_shared_down, L1_ffn_r_gate, L1_ffn_r_up, L1_ffn_r_down):

    def _L0_attn_ref(x, k1, k2, k3, a1, a2, b1, b2, c, value_weight, output_weight):
        import jax, jax.numpy as jnp
        import numpy as np
        B, N, W = (4, 512, 128)
        H, A, P = (16, 64, 64)
        n = jnp.linspace(0.0, 1.0, x.shape[-2])
        p1 = jnp.sum(jnp.sin(a1 * n + b1) * c, axis=-2)
        p2 = jnp.sum(jnp.sin(a2 * n + b2) * c, axis=-2)
        cross = jnp.einsum('bnw,hw->bhn', x, k1) + p1
        diag = jnp.einsum('bnw,hw->bhn', x, k2)
        extra = jnp.einsum('bnw,hw->bhn', x, k3)
        values = jnp.einsum('bnw,hwa->bhna', x, value_weight)
        cexp = lambda z: jnp.exp(jnp.clip(z, -20.0, 20.0))[..., None]
        cross, diag, extra = (cexp(cross), cexp(diag), cexp(extra))
        p2e = cexp(p2)
        num = jnp.cumsum(cross * values, axis=2) * p2e * extra + values * diag
        den = jnp.cumsum(cross, axis=2) * p2e * extra + diag
        out = num / den
        return jnp.einsum('bhna,hwa->bnw', out, output_weight)

    def _L0_ffn_ref(x, Wr, br, W1, b1, W2, b2):
        import jax, jax.numpy as jnp
        import numpy as np
        B, S, D, H, E = (4, 256, 128, 256, 8)
        d = x.shape[-1]
        tokens = x.reshape(-1, d)
        logits = tokens @ Wr + br
        probs = jax.nn.softmax(logits, axis=-1)
        expert = jnp.argmax(probs, axis=-1)
        max_prob = jnp.take_along_axis(probs, expert[:, None], axis=-1)
        h = jax.nn.relu(jnp.einsum('td,edh->teh', tokens, W1) + b1[None])
        y = jnp.einsum('teh,ehd->ted', h, W2) + b2[None]
        out = jnp.take_along_axis(y, expert[:, None, None], axis=1)[:, 0, :]
        return (out * max_prob).reshape(x.shape)

    def _L1_attn_ref(x, Wqkv, Wout, Wpos, coeffs):
        import jax, jax.numpy as jnp
        import numpy as np
        DIM = 128
        HEADS = 16
        HEAD_DIM = DIM // HEADS
        NUM_FILTERS = 4
        NUM_TAPS = 101
        RES = 64

        def _fir_fft(c, sig):
            R = sig.shape[0]
            L = R + c.shape[0] - 1
            out = jnp.fft.ifft(jnp.fft.fft(sig, n=L) * jnp.fft.fft(c, n=L)).real
            return out[:R]
        B, S, D = x.shape
        scale = HEAD_DIM ** (-0.5)
        proto = jnp.linspace(0.0, 1.0, RES).astype(x.dtype)
        table = jax.vmap(_fir_fft, in_axes=(0, None))(coeffs, proto).T
        r = jnp.arange(S)
        rel = jnp.abs(r[None, :] - r[:, None]).astype(jnp.float32) / max(S - 1, 1)
        idx = jnp.clip(jnp.round(rel * (RES - 1)).astype(jnp.int32), 0, RES - 1)
        pos_feat = table[idx]
        pos_bias = jnp.einsum('ijf,hf->hij', pos_feat, Wpos)
        qkv = jnp.einsum('bsd,ed->bse', x, Wqkv)
        q, k, v = jnp.split(qkv, 3, axis=-1)
        q = q.reshape(B, S, HEADS, HEAD_DIM)
        k = k.reshape(B, S, HEADS, HEAD_DIM)
        v = v.reshape(B, S, HEADS, HEAD_DIM)
        logits = jnp.einsum('bihd,bjhd->bhij', q, k) * scale + pos_bias[None]
        attn = jax.nn.softmax(logits, axis=-1)
        out = jnp.einsum('bhij,bjhd->bihd', attn, v).reshape(B, S, D)
        return jnp.einsum('bsd,ed->bse', out, Wout)

    def _L1_ffn_ref(hidden_states, gate_w, shared_gate, shared_up, shared_down, r_gate, r_up, r_down):
        import jax, jax.numpy as jnp
        import numpy as np
        B, S, H, F, E = (1, 256, 128, 256, 8)

        def _swiglu(x, wg, wu, wd):
            return jax.nn.silu(x @ wg.T) * (x @ wu.T) @ wd.T
        b, s, h = hidden_states.shape
        x = hidden_states.reshape(-1, h)
        shared_out = _swiglu(x, shared_gate, shared_up, shared_down)
        logits = x @ gate_w.T
        top_id = jnp.argmax(logits, axis=-1)
        score = jax.nn.sigmoid(jnp.max(logits, axis=-1))
        xs = x * score[:, None]

        def body(acc, ws):
            wg, wu, wd, e = ws
            xe = jnp.where((top_id == e)[:, None], xs, 0.0)
            return (acc + _swiglu(xe, wg, wu, wd), None)
        acc0 = jnp.zeros_like(x)
        routed_out, _ = jax.lax.scan(body, acc0, (r_gate, r_up, r_down, jnp.arange(E)))
        return (shared_out + routed_out).reshape(b, s, h)
    x = L0_attn_x
    x = _layernorm(x + _L0_attn_ref(x, L0_attn_k1, L0_attn_k2, L0_attn_k3, L0_attn_a1, L0_attn_a2, L0_attn_b1, L0_attn_b2, L0_attn_c, L0_attn_value_weight, L0_attn_output_weight), axis=-1)
    x = _layernorm(x + _L0_ffn_ref(x, L0_ffn_Wr, L0_ffn_br, L0_ffn_W1, L0_ffn_b1, L0_ffn_W2, L0_ffn_b2), axis=-1)
    x = _layernorm(x + _L1_attn_ref(x, L1_attn_Wqkv, L1_attn_Wout, L1_attn_Wpos, L1_attn_coeffs), axis=-1)
    x = _layernorm(x + _L1_ffn_ref(x, L1_ffn_gate_w, L1_ffn_shared_gate, L1_ffn_shared_up, L1_ffn_shared_down, L1_ffn_r_gate, L1_ffn_r_up, L1_ffn_r_down), axis=-1)
    return x

_drawn_inputs = setup_inputs


def setup_inputs(seed=0):
    import zlib

    import numpy as np

    out = dict(_drawn_inputs(seed))
    spreads = {'L0_ffn_br': (0.0, 0.1), 'L0_ffn_b1': (0.0, 0.418), 'L0_ffn_b2': (0.0, 0.1)}
    factors = {'L0_attn_a1': 8.0,
     'L0_attn_a2': 25.719,
     'L0_attn_b1': 8.0,
     'L0_attn_b2': 8.0,
     'L0_attn_c': 8.0,
     'L1_attn_coeffs': 2.94}
    for name, (base, spread) in spreads.items():
        noise = np.random.default_rng([zlib.crc32(name.encode()), seed]).standard_normal(out[name].shape)
        drawn = base * np.exp(spread * noise) if base else spread * noise
        out[name] = jnp.asarray(drawn.astype(out[name].dtype))
    for name, factor in factors.items():
        out[name] = (out[name] * factor).astype(out[name].dtype)
    return out
```

```python
from contextlib import ExitStack

import concourse.bass as bass
from concourse import mybir

F32 = mybir.dt.float32
BF16 = mybir.dt.bfloat16
U32 = mybir.dt.uint32
I32 = mybir.dt.int32
ALU = mybir.AluOpType
ACT = mybir.ActivationFunctionType
AX = mybir.AxisListType.X

P = 128
NB, N, W = 16, 512, 128
T = N // P
H, A = 16, 64
HA = H * A
SP_ = 64
E = 8
FH = 256
TAPS, RES, NF = 101, 64, 4
HD = W // H
DELTA = 2 * T - 1
UPAD = 2 * P
REGION = NB * N + P
BLOCKS = NB * T + E - 1
BLOCKS += BLOCKS % 2
SPARE = E * REGION
ROWS = SPARE + E * P
EPS = 1e-5
TWO_PI = 6.283185307179586
ROUND = 12582912.0
LIMIT = 20.0
A_OWN = 84
C_OWN = 110
C_POOL = 12
E_OWN = 36


class Step:

    def __init__(self, b, half, par, mod=2):
        self.b, self.half, self.par, self.mod = b, half, par, mod

    def back(self, n=1):
        s = self
        for _ in range(n):
            s = Step(s.b - 1, s.half if s.par else s.half - 1, (s.par - 1) % s.mod, s.mod)
        return s

    def ahead(self):
        last = self.par == self.mod - 1
        return Step(self.b + 1, self.half + 1 if last else self.half, (self.par + 1) % self.mod, self.mod)


def at(b, mod=2):
    return Step(b, b // mod, b % mod, mod)


def steps(i, first, mod=2):
    return [Step(i * mod + (first + j), i + first // mod, j, mod) for j in range(mod)]


def need(eng, sem, n):
    if not (isinstance(n, int) and n <= 0):
        eng.wait_ge(sem, n)


def apart(eng, passed):
    eng.sem_inc(passed, 1)


class Own:

    def __init__(self, eng, sem, passed=None):
        self.eng, self.sem, self.passed = eng, sem, passed
        self.start, self.n, self.i, self.per = 0, 0, None, 0

    def did(self, ins):
        ins.then_inc(self.sem, 1)
        self.n += 1

    def wait(self, alone=False):
        done = self.start + self.n
        if self.i is not None:
            done = self.i * self.per + done
        need(self.eng, self.sem, done)
        if alone:
            apart(self.eng, self.passed)

    def enter(self, i, per):
        self.start, self.n, self.i, self.per = self.start + self.n, 0, i, per

    def leave(self, trips):
        assert self.n == self.per, f"signals of a pass: {self.n}, not {self.per}"
        self.start, self.n, self.i = self.start + self.per * trips, 0, None


def layer_norm(v, own, src, dst, st, mv, ve, var_ready, rstd_ready, rstd, n, done):
    for t in range(T):
        own.did(v.bn_stats(st[:, t, :], src[:, t, :]))
    own.wait(alone=True)
    for t in range(T):
        own.did(v.bn_aggr(mv[:, t, :], st[:, t, :]))
    own.wait()
    v.tensor_scalar(ve[:], mv[:, :, 1], EPS, None, ALU.add).then_inc(var_ready, 1)
    v.wait_ge(rstd_ready, n)
    for t in range(T):
        ins = v.tensor_scalar(dst[:, t, :], src[:, t, :], mv[:, t, 0:1], rstd[:, t:t + 1], ALU.subtract, ALU.mult)
    ins.then_inc(done, 1)


def route(v, own, k, lg, top, idx, idxf, oh):
    apart(own.eng, own.passed)
    for t in range(T):
        own.did(v.max(top[:, t, :], lg[:, t, :]))
    own.wait(alone=True)
    for t in range(T):
        own.did(v.max_index(idx[:, t, :], top[:, t, :], lg[:, t, :]))
    own.wait()
    own.did(v.tensor_copy(idxf[:], idx[:, :, 0]))
    own.wait()


def slots_of(v, own, k, runs, run, oh, before, total, sel, slotf):
    own.did(v.tensor_copy(runs[:, 0, :], run[:]))
    own.wait()
    for t in range(T):
        dst = runs[:, t + 1, :] if t < T - 1 else run[:]
        own.did(v.tensor_tensor(dst, total[:, t, :], runs[:, t, :], ALU.add))
        own.wait()
    own.did(v.tensor_tensor(sel[:], before, runs[:], ALU.add))
    own.wait()
    own.did(v.tensor_tensor(sel[:], sel[:], oh[:], ALU.mult))
    own.wait()
    own.did(v.tensor_reduce(slotf[:], sel[:], AX, ALU.add))
    own.wait()


def attention_one(nc, g, keep):
    io, sem = g.io, g.sem
    with ExitStack() as ctx:
        def sb(name, shape, dt=F32):
            return ctx.enter_context(nc.sbuf_tensor(name, shape, dt))

        bank = [ctx.enter_context(nc.psum_tensor(f"a_bank{i}", [P, 512], F32)) for i in range(8)]
        v_ps, t_ps, base_ps, small, xt_ps, y_ps = bank[0:2], bank[2:4], bank[4], bank[5], bank[6], bank[7]
        lg_ps = small[:, 0:192].rearrange("p (t k) -> p t k", t=T)
        cb_ps = small[:, 192:208]
        rl_ps = small[:, 208:240].rearrange("p (t e) -> p t e", t=T)
        before_ps = small[:, 240:272].rearrange("p (t e) -> p t e", t=T)
        total_ps = small[:, 272:304].rearrange("p (t e) -> p t e", t=T)

        wk = sb("wk", [P, 3 * H])
        wv = sb("wv", [P, HA])
        wo = sb("wo", [P, HA // P, W])
        wr = sb("wr", [P, E])
        br = sb("br", [P, E])
        xT = [sb(f"xT{i}", [P, T, P]) for i in range(2)]
        xtok = [sb(f"xtok{i}", [P, T, W]) for i in range(2)]
        p1 = sb("p1", [P, T, H])
        ep2 = sb("ep2", [P, T, H])
        z = sb("z", [P, T, 3 * H])
        ez = sb("ez", [P, T, 3 * H])
        gt = sb("gt", [P, T, H])
        dg = sb("dg", [P, T, H])
        qc = sb("qc", [P, T, H])
        sumc = sb("sumc", [P, T, H])
        r = sb("r", [P, T, H])
        vp = [sb(f"vp{i}", [P, HA]) for i in range(2)]
        v2 = [sb(f"v2{i}", [P, HA]) for i in range(2)]
        q = sb("q", [P, T, HA])
        s1 = [sb(f"s1{i}", [P, T, HA]) for i in range(2)]
        base = sb("base", [P, HA])
        o = [sb(f"o{i}", [P, HA]) for i in range(2)]
        oT = [sb(f"oT{i}", [P, HA // P, P]) for i in range(2)]
        xr = sb("xr", [P, T, W])
        st = sb("st", [P, T, 6])
        mv = sb("mv", [P, T, 2])
        ve = sb("ve", [P, T])
        rstd = sb("rstd", [P, T])
        x1 = [sb(f"x1{i}", [P, T, W]) for i in range(2)]
        x1T = sb("x1T", [P, T, P])
        rl = sb("rl", [P, T, E])
        rsh = sb("rsh", [P, T, E])
        rex = sb("rex", [P, T, E])
        rsum = sb("rsum", [P, T])
        top = sb("top", [P, T, 8])
        idx = sb("idx", [P, T, 8], U32)
        idxf = sb("idxf", [P, T])
        oh = sb("oh", [P, T, E])
        runs = sb("runs", [P, T, E])
        sel = sb("sel", [P, T, E])
        slotf = sb("slotf", [P, T])
        slot = [sb(f"slot{i}", [P, T], U32) for i in range(2)]
        amp = sb("amp", [P, 5, H * SP_ // P])
        turns = sb("turns", [P, 4, H * SP_ // P])
        pos = sb("pos", [P, N])
        hmask = sb("hmask", [P, H * SP_ // P, H])
        cm = sb("cm", [P, H * SP_ // P, H])
        ph = [sb(f"ph{i}", [P, N]) for i in range(2)]
        rnd = [sb(f"rnd{i}", [P, N]) for i in range(2)]
        frac = [sb(f"frac{i}", [P, N]) for i in range(2)]
        sine = [sb(f"sine{i}", [P, N]) for i in range(2)]
        coeffs = sb("coeffs", [TAPS, NF])
        ramp = sb("ramp", [TAPS, RES])
        wpos = sb("wpos", [NF, H])
        table = sb("table", [NF, RES])
        levels = sb("levels", [RES, H])
        onehot = sb("onehot", [RES, DELTA * UPAD])
        line = sb("line", [H, DELTA * UPAD])
        SB = H * SP_ // P
        C4 = DELTA * UPAD // 4

        with nc.Block() as block:

            @block.sync
            def _(sp):
                for dst, src in ((amp, "sines"), (pos, "pos"), (hmask, "hmask")):
                    sp.dma_start(dst[:], io[src]).then_inc(sem("sines_in"), 16)
                for dst, src in ((wk, "wk"), (wv, "wv"), (keep.ident, "ident")):
                    sp.dma_start(dst[:], io[src]).then_inc(sem("wv_in"), 16)

                def load(s):
                    need(sp, sem("v_ready"), 8 * (s.b - 1))
                    sp.dma_start(xT[s.par][:], io["xT"][bass.ds(s.b, 1)].rearrange("o w t p -> w (o t) p")
                                 ).then_inc(sem(f"xT_in{s.par}"), 16)
                    need(sp, sem("y_read"), s.b - 1)
                    sp.dma_start(xtok[s.par][:], io["x"][bass.ds(s.b, 1)].rearrange("o p t w -> p (o t) w")
                                 ).then_inc(sem(f"xtok_in{s.par}"), 16)

                def store(s):
                    sp.wait_ge(sem("x1_ready"), s.b + 1)
                    sp.dma_start(io["x1_d"][bass.ds(s.b, 1)].rearrange("o p t w -> p (o t) w"), x1[s.par][:]
                                 ).then_inc(sem(f"x1_out{s.par}"), 16)

                load(at(0))
                load(at(1))
                for dst, src in ((keep.tri, "tri"), (wo, "wo"), (wr, "wr"), (br, "br"), (keep.iota, "iota"),
                                 (keep.run, "run0")):
                    sp.dma_start(dst[:], io[src]).then_inc(sem("wo_in"), 16)
                for dst, src in ((coeffs, "coeffs"), (ramp, "ramp"), (wpos, "wpos"), (onehot, "onehot")):
                    sp.dma_start(dst[:], io[src]).then_inc(sem("bias_in"), 16)
                sp.wait_ge(sem("line_ready"), 4)
                sp.dma_start(io["line_d"], line[:]).then_inc(sem("line_out"), 16)
                sp.wait_ge(sem("line_out"), 16)
                for h in range(H):
                    src = bass.AP(io["line_d"].tensor, h * DELTA * UPAD + P - 1, [[UPAD, DELTA], [-1, P], [1, P]])
                    sp.dma_start(io["bias_d"][h].rearrange("p d q -> d p q"), src).then_inc(sem("bias_out"), 16)
                with sp.Fori(0, NB // 2 - 1) as i:
                    for s in steps(i, 2):
                        load(s)
                        store(s.back(2))
                store(at(NB - 2))
                store(at(NB - 1))
                sp.wait_ge(sem("x1_out0"), 16 * NB // 2)
                sp.wait_ge(sem("x1_out1"), 16 * NB // 2)

            @block.tensor
            def _(pe):
                pe.wait_ge(sem("sines_in"), 48)
                for k in range(2 * SB):
                    pe.wait_ge(sem("sine_ready"), k + 1)
                    if k == 0:
                        pe.wait_ge(sem("cm_ready"), SB)
                    for t in range(T):
                        mm = nc.tensor.matmul(y_ps[:, (k // SB * T + t) * H:(k // SB * T + t + 1) * H],
                                              sine[k % 2][:, t * P:(t + 1) * P], cm[:, k % SB, :],
                                              start=(k == 0 and t == 0), stop=(k % SB == SB - 1),
                                              skip_group_check=True)
                    mm.then_inc(sem("pos_sum"), 1)
                pe.wait_ge(sem("bias_in"), 64)
                nc.tensor.matmul(base_ps[0:NF, 0:RES], coeffs[:], ramp[:], start=True, stop=True).then_inc(sem("table_ps"), 1)
                pe.wait_ge(sem("table_sb"), 1)
                nc.tensor.matmul(xt_ps[0:RES, 0:H], table[:], wpos[:], start=True, stop=True).then_inc(sem("table_ps"), 1)
                pe.wait_ge(sem("table_sb"), 2)
                for c in range(4):
                    if c >= 1:
                        pe.wait_ge(sem("line_ready"), c)
                    nc.tensor.matmul(xt_ps[0:H, 0:C4], levels[:], onehot[:, c * C4:(c + 1) * C4], start=True,
                                     stop=True).then_inc(sem("line_ps"), 1)
                pe.wait_ge(sem("line_ready"), 4)
                pe.wait_ge(sem("wv_in"), 48)

                def front_logits(s):
                    pe.wait_ge(sem(f"xT_in{s.par}"), 16 * s.half + 16)
                    for t in range(T):
                        mm = nc.tensor.matmul(lg_ps[:, t, :], xT[s.par][:, t, :], wk[:], start=True, stop=True)
                    mm.then_inc(sem("lg_ready"), 1)

                def front_values(s, t):
                    for h in range(2):
                        need(pe, sem("v2_ready"), 8 * s.b + 2 * t + h - 1)
                        nc.tensor.matmul(v_ps[h][:], xT[s.par][:, t, :], wv[:, 512 * h:512 * h + 512],
                                         start=True, stop=True).then_inc(sem("v_ready"), 1)

                def back_base(s):
                    pe.wait_ge(sem("q_ready"), 3 * s.b + 3)
                    for h in range(2):
                        need(pe, sem("base_taken"), 2 * s.b + h)
                        nc.tensor.matmul(base_ps[:], keep.tri[:], q[:, T - 1, 512 * h:512 * h + 512],
                                         start=True, stop=True).then_inc(sem("base_ready"), 1)
                    need(pe, sem("count_read"), s.b - 1)
                    nc.tensor.matmul(cb_ps, keep.tri[:], qc[:, T - 1, :], start=True, stop=True
                                     ).then_inc(sem("cbase_ready"), 1)

                def back_turn(s, t):
                    pe.wait_ge(sem("o_ready"), 4 * s.b + t + 1)
                    for h in range(2):
                        need(pe, sem("turn_taken"), 8 * s.b + 2 * t + h - 1)
                        for k in range(4):
                            c = (4 * h + k) * P
                            mm = nc.tensor.transpose(t_ps[h][:, k * P:(k + 1) * P], o[t % 2][:, c:c + P], keep.ident[:])
                        mm.then_inc(sem("turn_ready"), 1)

                def back_out(s, t):
                    if t == 0:
                        need(pe, sem("y_read"), s.b)
                    pe.wait_ge(sem("turn_taken"), 8 * s.b + 2 * t + 2)
                    for k in range(HA // P):
                        mm = nc.tensor.matmul(y_ps[:, t * W:(t + 1) * W], oT[t % 2][:, k, :], wo[:, k, :],
                                              start=(k == 0), stop=(k == HA // P - 1))
                    mm.then_inc(sem("y_ready"), 1)

                def route_turn(s):
                    pe.wait_ge(sem("x1_ready"), s.b + 1)
                    need(pe, sem("x1T_taken"), s.b)
                    for t in range(T):
                        mm = nc.tensor.transpose(xt_ps[:, t * P:(t + 1) * P], x1[s.par][:, t, :], keep.ident[:])
                    mm.then_inc(sem("x1T_ready"), 1)

                def route_logits(s):
                    pe.wait_ge(sem("x1T_taken"), s.b + 1)
                    for t in range(T):
                        mm = nc.tensor.matmul(rl_ps[:, t, :], x1T[:, t, :], wr[:], start=True, stop=True)
                    mm.then_inc(sem("rl_ready"), 1)

                def route_count(s):
                    pe.wait_ge(sem("oh_ready"), s.b + 1)
                    nc.tensor.matmul(before_ps, keep.tri[:], oh[:], start=True, stop=True)
                    nc.tensor.matmul(total_ps, keep.ones[:], oh[:], start=True, stop=True).then_inc(sem("count_ready"), 1)

                def step(s, front=True, back=True, routing=True):
                    if back:
                        back_base(s.back())
                    if front:
                        if back:
                            pe.wait_ge(sem("cbase_read"), s.b)
                        front_logits(s)
                    if routing:
                        route_turn(s.back(2))
                    for t in range(T):
                        if back:
                            back_turn(s.back(), t)
                        if front:
                            front_values(s, t)
                        if back:
                            back_out(s.back(), t)
                        if routing and t == 0:
                            if front:
                                pe.wait_ge(sem("lg_read"), s.b + 1)
                            elif back:
                                pe.wait_ge(sem("cbase_read"), s.b)
                            route_logits(s.back(2))
                        if routing and t == 2:
                            route_count(s.back(2))

                pe.wait_ge(sem("pos_read"), 2)
                pe.wait_ge(sem("wo_in"), 96)
                pe.wait_ge(sem("const_ready"), 2)
                step(at(0), back=False, routing=False)
                step(at(1), routing=False)
                with pe.Fori(0, NB // 2 - 1) as i:
                    for s in steps(i, 2):
                        step(s)
                step(at(NB), front=False)
                step(at(NB + 1), front=False, back=False)

            @block.scalar
            def _(act):
                for k in range(2 * SB):
                    act.wait_ge(sem("frac_ready"), k + 1)
                    need(act, sem("pos_sum"), k - 1)
                    nc.scalar.activation(sine[k % 2][:], frac[k % 2][:], ACT.Sin, scale=TWO_PI * (1 - 2e-7)
                                         ).then_inc(sem("sine_ready"), 1)
                act.wait_ge(sem("pos_read"), 2)
                nc.scalar.activation(ep2[:], gt[:], ACT.Exp).then_inc(sem("ep2_ready"), 1)

                def back_base(s):
                    need(act, sem("o_ready"), 4 * s.b)
                    for h in range(2):
                        act.wait_ge(sem("base_ready"), 2 * s.b + h + 1)
                        nc.scalar.copy(base[:, 512 * h:512 * h + 512], base_ps[:]).then_inc(sem("base_taken"), 1)

                def front_exp(s):
                    act.wait_ge(sem("lg_read"), s.b + 1)
                    need(act, sem("vp_ready"), 8 * s.b)
                    nc.scalar.activation(ez[:], z[:], ACT.Exp).then_inc(sem("ez_ready"), 1)

                def front_own(s, t):
                    if t == 0:
                        act.wait_ge(sem("dg_ready"), s.b + 1)
                    need(act, sem("s1_ready"), 4 * s.b + t - 1)
                    for half in range(2):
                        act.wait_ge(sem("vp_ready"), 8 * s.b + 2 * t + half + 1)
                        for k in range(H // 2):
                            h = H // 2 * half + k
                            ins = nc.scalar.activation(v2[t % 2][:, h * A:(h + 1) * A], v_ps[half][:, k * A:(k + 1) * A],
                                                       ACT.Copy, scale=dg[:, t, h:h + 1])
                        ins.then_inc(sem("v2_ready"), 1)

                def back_turn(s, t):
                    need(act, sem("y_ready"), 4 * s.b + t - 1)
                    for h in range(2):
                        act.wait_ge(sem("turn_ready"), 8 * s.b + 2 * t + h + 1)
                        nc.scalar.copy(oT[t % 2][:, 4 * h:4 * h + 4, :], t_ps[h][:].rearrange("p (k n) -> p k n", k=4)
                                       ).then_inc(sem("turn_taken"), 1)

                def route_turn(s):
                    act.wait_ge(sem("x1T_ready"), s.b + 1)
                    need(act, sem("rl_ready"), s.b)
                    nc.scalar.copy(x1T[:], xt_ps[:].rearrange("p (t n) -> p t n", t=T)).then_inc(sem("x1T_taken"), 1)

                def route_exp(s):
                    act.wait_ge(sem("rsh_ready"), s.b + 1)
                    nc.scalar.activation(rex[:], rsh[:], ACT.Exp).then_inc(sem("rex_ready"), 1)

                def step(s, front=True, back=True, routing=True):
                    if back:
                        back_base(s.back())
                    if front:
                        front_exp(s)
                    if routing:
                        route_turn(s.back(2))
                    for t in range(T):
                        if back:
                            back_turn(s.back(), t)
                        if front:
                            front_own(s, t)
                        if routing and t == 1:
                            route_exp(s.back(2))

                step(at(0), back=False, routing=False)
                step(at(1), routing=False)
                with act.Fori(0, NB // 2 - 1) as i:
                    for s in steps(i, 2):
                        step(s)
                step(at(NB), front=False)
                step(at(NB + 1), front=False, back=False)

            @block.gpsimd
            def _(pool):
                nc.gpsimd.memset(keep.ones[:], 1.0).then_inc(sem("const_ready"), 1)
                nc.gpsimd.memset(keep.minus_half[:], -0.5).then_inc(sem("const_ready"), 1)

                def front_sums(s, t):
                    if t == 0:
                        pool.wait_ge(sem("vp_ready"), 8 * s.b + 2)
                    else:
                        pool.wait_ge(sem("vp_ready"), 8 * s.b + 2 * t + 2)
                        if t == T - 1:
                            need(pool, sem("base_ready"), 2 * s.b)
                        if t >= 2:
                            pool.wait_ge(sem("q_ready"), 3 * s.b + t - 1)
                        nc.gpsimd.tensor_tensor(q[:, t, :], q[:, t - 1, :], vp[t % 2][:], ALU.add
                                                ).then_inc(sem("q_ready"), 1)
                        pool.wait_ge(sem("q_ready"), 3 * s.b + t)
                    pool.wait_ge(sem("v2_ready"), 8 * s.b + 2 * t + 2)
                    need(pool, sem("o_ready"), 4 * (s.b - 1))
                    nc.gpsimd.tensor_tensor(s1[s.par][:, t, :], q[:, t, :], v2[t % 2][:], ALU.add
                                            ).then_inc(sem("s1_ready"), 1)

                def back_rstd(s):
                    pool.wait_ge(sem("var_ready"), s.b + 1)
                    nc.gpsimd.tensor_tensor(rstd[:], ve[:], keep.minus_half[:], ALU.pow).then_inc(sem("rstd_ready"), 1)

                def route_scatter(s):
                    pool.wait_ge(sem("slot_ready"), s.b + 1)
                    apart(pool, sem("pool_passed"))
                    for t in range(T):
                        pool.indirect_dma_start(
                            out=io["xs_d"], out_offset=bass.IndirectOffsetOnAxis(ap=slot[s.par][:, t:t + 1], axis=0),
                            in_=x1[s.par][:, t, :], in_offset=None).then_inc(sem(f"scat{s.par}"), 16)

                def step(s, front=True, back=True, routing=True):
                    if front:
                        for t in range(T):
                            front_sums(s, t)
                    if routing:
                        route_scatter(s.back(2))
                    if back:
                        back_rstd(s.back())

                pool.wait_ge(sem("const_ready"), 2)
                step(at(0), back=False, routing=False)
                step(at(1), routing=False)
                pool.wait_ge(sem("bias_out"), 16 * H)
                for h in range(H):
                    pool.dma_start(keep.bias[:, h, :, :], io["bias_d"][h]).then_inc(sem("bias_ready"), 16)
                with pool.Fori(0, NB // 2 - 1) as i:
                    for s in steps(i, 2):
                        step(s)
                step(at(NB), front=False)
                step(at(NB + 1), front=False, back=False)
                pool.wait_ge(sem("scat0"), 16 * T * NB // 2)
                pool.wait_ge(sem("scat1"), 16 * T * NB // 2)
                pool.wait_ge(sem("bias_ready"), 16 * H)

            @block.vector
            def _(dve):
                v = nc.vector
                own = Own(dve, sem("a_own"), sem("dve_passed"))
                dve.wait_ge(sem("sines_in"), 48)
                own.did(v.tensor_scalar(turns[:], amp[:, 0:4, :], 1.0 / TWO_PI, None, ALU.mult))
                for k in range(SB):
                    v.tensor_scalar(cm[:, k, :], hmask[:, k, :], amp[:, 4, k:k + 1], None, ALU.mult).then_inc(sem("cm_ready"), 1)
                for k in range(2 * SB):
                    which, blk, b = k // SB, k % SB, k % 2
                    own.wait()
                    own.did(v.tensor_scalar(ph[b][:], pos[:], turns[:, which, blk:blk + 1],
                                            turns[:, 2 + which, blk:blk + 1], ALU.mult, ALU.add))
                    own.wait()
                    own.did(v.tensor_scalar(rnd[b][:], ph[b][:], ROUND, ROUND, ALU.add, ALU.subtract))
                    own.wait()
                    need(dve, sem("sine_ready"), k - 1)
                    v.tensor_tensor(frac[b][:], ph[b][:], rnd[b][:], ALU.subtract).then_inc(sem("frac_ready"), 1)
                dve.wait_ge(sem("pos_sum"), 2 * SB)
                v.tensor_copy(p1[:].rearrange("p t h -> p (t h)"), y_ps[:, 0:T * H]).then_inc(sem("pos_read"), 1)
                v.tensor_scalar(gt[:].rearrange("p t h -> p (t h)"), y_ps[:, T * H:2 * T * H], -LIMIT, LIMIT, ALU.max, ALU.min
                                ).then_inc(sem("pos_read"), 1)
                dve.wait_ge(sem("table_ps"), 1)
                v.tensor_copy(table[:], base_ps[0:NF, 0:RES]).then_inc(sem("table_sb"), 1)
                dve.wait_ge(sem("table_ps"), 2)
                v.tensor_copy(levels[:], xt_ps[0:RES, 0:H]).then_inc(sem("table_sb"), 1)
                for c in range(4):
                    dve.wait_ge(sem("line_ps"), c + 1)
                    v.tensor_copy(line[:, c * C4:(c + 1) * C4], xt_ps[0:H, 0:C4]).then_inc(sem("line_ready"), 1)
                dve.wait_ge(sem("ep2_ready"), 1)
                dve.wait_ge(sem("wo_in"), 96)

                def heads(x):
                    return x.rearrange("p (h a) -> p h a", a=A)

                def back_den(s):
                    dve.wait_ge(sem("cbase_ready"), s.b + 1)
                    own.did(v.tensor_tensor(gt[:], cb_ps.unsqueeze(1).to_broadcast([P, T, H]), sumc[:], ALU.add))
                    own.wait()
                    v.reciprocal(r[:], gt[:]).then_inc(sem("cbase_read"), 1)

                def front_weights(s):
                    dve.wait_ge(sem("lg_ready"), s.b + 1)
                    need(dve, sem("ez_ready"), s.b)
                    own.did(v.tensor_tensor(z[:, :, 0:H], lg_ps[:, :, 0:H], p1[:], ALU.add))
                    own.did(v.tensor_scalar(z[:, :, H:3 * H], lg_ps[:, :, H:3 * H], -LIMIT, LIMIT, ALU.max, ALU.min))
                    own.wait()
                    v.tensor_scalar(z[:, :, 0:H], z[:, :, 0:H], -LIMIT, LIMIT, ALU.max, ALU.min).then_inc(sem("lg_read"), 1)
                    dve.wait_ge(sem("ez_ready"), s.b + 1)
                    own.did(v.tensor_tensor(gt[:], ez[:, :, 2 * H:3 * H], ep2[:], ALU.mult))
                    own.did(v.tensor_copy(qc[:, 0, :], ez[:, 0, 0:H]))
                    own.wait()
                    own.did(v.reciprocal(gt[:], gt[:]))
                    for t in range(1, T):
                        own.did(v.tensor_tensor(qc[:, t, :], qc[:, t - 1, :], ez[:, t, 0:H], ALU.add))
                        own.wait()
                    need(dve, sem("v2_ready"), 8 * s.b)
                    v.tensor_tensor(dg[:], gt[:], ez[:, :, H:2 * H], ALU.mult).then_inc(sem("dg_ready"), 1)
                    dve.wait_ge(sem("dg_ready"), s.b + 1)
                    own.did(v.tensor_tensor(sumc[:], qc[:], dg[:], ALU.add))

                def front_values(s, t):
                    if t == 0:
                        need(dve, sem("s1_ready"), 4 * s.b)
                    else:
                        need(dve, sem("q_ready"), 3 * s.b + t - 2)
                    dst = q[:, 0, :] if t == 0 else vp[t % 2][:]
                    for h in range(2):
                        dve.wait_ge(sem("v_ready"), 8 * s.b + 2 * t + h + 1)
                        c = ez[:, t, h * H // 2:(h + 1) * H // 2].unsqueeze(2).to_broadcast([P, H // 2, A])
                        v.tensor_tensor(heads(dst[:, 512 * h:512 * h + 512]), heads(v_ps[h][:]), c, ALU.mult
                                        ).then_inc(sem("vp_ready"), 1)

                def back_heads(s, t):
                    dve.wait_ge(sem("s1_ready"), 4 * s.b + t + 1)
                    if t == 0:
                        dve.wait_ge(sem("base_taken"), 2 * s.b + 2)
                        dve.wait_ge(sem("cbase_read"), s.b + 1)
                    need(dve, sem("turn_ready"), 8 * s.b + 2 * t - 2)
                    own.did(v.tensor_tensor(o[t % 2][:], base[:], s1[s.par][:, t, :], ALU.add))
                    own.wait()
                    v.tensor_tensor(heads(o[t % 2][:]), heads(o[t % 2][:]), r[:, t, :].unsqueeze(2).to_broadcast([P, H, A]),
                                    ALU.mult).then_inc(sem("o_ready"), 1)

                def back_norm(s):
                    dve.wait_ge(sem("y_ready"), 4 * s.b + 4)
                    dve.wait_ge(sem(f"xtok_in{s.par}"), 16 * s.half + 16)
                    v.tensor_tensor(xr[:].rearrange("p t w -> p (t w)"), y_ps[:],
                                    xtok[s.par][:].rearrange("p t w -> p (t w)"), ALU.add).then_inc(sem("y_read"), 1)
                    dve.wait_ge(sem("y_read"), s.b + 1)
                    need(dve, sem(f"x1_out{s.par}"), 16 * s.half)
                    need(dve, sem(f"scat{s.par}"), 16 * T * s.half)
                    layer_norm(v, own, xr, x1[s.par], st, mv, ve, sem("var_ready"), sem("rstd_ready"), rstd, s.b + 1,
                               sem("x1_ready"))

                def route_choose(s):
                    dve.wait_ge(sem("rl_ready"), s.b + 1)
                    own.did(v.tensor_tensor(rl[:], rl_ps, br[:].unsqueeze(1).to_broadcast([P, T, E]), ALU.add))
                    own.wait()
                    route(v, own, keep, rl, top, idx, idxf, oh)
                    need(dve, sem("rex_ready"), s.b)
                    v.tensor_tensor(rsh[:], rl[:], top[:, :, 0:1].to_broadcast([P, T, E]), ALU.subtract).then_inc(sem("rsh_ready"), 1)
                    v.tensor_tensor(oh[:], keep.iota[:].unsqueeze(1).to_broadcast([P, T, E]),
                                    idxf[:].unsqueeze(2).to_broadcast([P, T, E]), ALU.is_equal).then_inc(sem("oh_ready"), 1)

                def route_slots(s):
                    dve.wait_ge(sem("rex_ready"), s.b + 1)
                    own.did(v.tensor_reduce(rsum[:], rex[:], AX, ALU.add))
                    dve.wait_ge(sem("count_ready"), s.b + 1)
                    dve.wait_ge(sem("oh_ready"), s.b + 1)
                    slots_of(v, own, keep, runs, keep.run, oh, before_ps, total_ps, sel, slotf)
                    v.reciprocal(keep.prob[:, bass.ds(T * s.b, T)], rsum[:]).then_inc(sem("count_read"), 1)
                    need(dve, sem(f"scat{s.par}"), 16 * T * s.half)
                    own.did(v.tensor_copy(keep.slots[:, bass.ds(T * s.b, T)], slotf[:]))
                    v.tensor_copy(slot[s.par][:], slotf[:]).then_inc(sem("slot_ready"), 1)

                def step(s, front=True, back=True, routing=True):
                    if back:
                        back_den(s.back())
                    if front:
                        front_weights(s)
                    if back:
                        back_heads(s.back(), 0)
                    for t in range(T):
                        if front:
                            front_values(s, t)
                        if back and t < T - 1:
                            back_heads(s.back(), t + 1)
                        if routing and t == 1:
                            route_choose(s.back(2))
                        if routing and t == 3:
                            route_slots(s.back(2))
                    if back:
                        back_norm(s.back())

                step(at(0), back=False, routing=False)
                step(at(1), routing=False)
                with dve.Fori(0, NB // 2 - 1) as i:
                    own.enter(i, A_OWN)
                    for s in steps(i, 2):
                        step(s)
                own.leave(NB // 2 - 1)
                step(at(NB), front=False)
                step(at(NB + 1), front=False, back=False)


def experts(nc, g, keep, tag, src, dst, w_in, w_out, b_in=None, b_out=None):
    io = g.io
    gated = b_in is None
    wide = 2 * FH if gated else FH

    def sem(name):
        return g.sem(f"{tag}_{name}")

    with ExitStack() as ctx:
        def sb(name, shape, dt=F32):
            return ctx.enter_context(nc.sbuf_tensor(f"{tag}_{name}", shape, dt))

        bank = [ctx.enter_context(nc.psum_tensor(f"{tag}_bank{i}", [P, 512], F32)) for i in range(8)]
        xT_ps, h_ps, hT_ps, y_ps = bank[0:2], bank[2:4], bank[4:6], bank[6:8]
        wi = sb("wi", [P, E, wide])
        wo = sb("wo", [P, E, 2, W])
        if not gated:
            bi = sb("bi", [P, E, FH])
            bo = sb("bo", [P, E, W])
        zeros = sb("zeros", [P, W])
        lane = sb("lane", [P, 1])
        turn = sb("turn", [P, BLOCKS])
        count = sb("count", [P, E])
        blocks = sb("blocks", [P, E])
        ones8 = sb("ones8", [P, E])
        ends = sb("ends", [P, E])
        offs = sb("offs", [P, E])
        padf = sb("padf", [P, E])
        pad = [sb(f"pad{e}", [P, 1], U32) for e in range(E)]
        past = sb("past", [P, BLOCKS, E])
        ef = sb("ef", [P, BLOCKS])
        isf = sb("isf", [P, BLOCKS, E])
        rowf = sb("rowf", [P, BLOCKS])
        chosen = sb("chosen", [P, NB * T])
        spare = sb("spare", [P, BLOCKS])
        row = sb("row", [P, BLOCKS], I32)
        expert = sb("expert", [P, BLOCKS], I32)
        x = [sb(f"x{i}", [P, W]) for i in range(4)]
        xT = [sb(f"xT{i}", [P, P]) for i in range(2)]
        gate = [sb(f"gate{i}", [P, FH]) for i in range(2)]
        h = [sb(f"h{i}", [P, FH]) for i in range(2)]
        hT = [sb(f"hT{i}", [P, 2, P]) for i in range(2)]
        y = [sb(f"y{i}", [P, W]) for i in range(4)]

        def loop(eng, step):
            for k in range(4):
                step(at(k, 4), [k >= n for n in range(4)])
            with eng.Fori(0, BLOCKS // 4 - 1) as i:
                for s in steps(i, 4, 4):
                    step(s, [True] * 4)
            for k in range(BLOCKS, BLOCKS + 3):
                step(at(k, 4), [k - n < BLOCKS for n in range(4)])

        def which(eng, table, s, top):
            return eng.value_load(table[0:1, bass.ds(s.b, 1)], min_val=0, max_val=top)

        with nc.Block() as block:

            @block.sync
            def _(sp):
                for d, name in ((lane, "lane"), (turn, "turn")):
                    sp.dma_start(d[:], io[name]).then_inc(sem("lane_in"), 16)
                sp.dma_start(wi[:], io[w_in]).then_inc(sem("wi_in"), 16)
                sp.dma_start(wo[:], io[w_out]).then_inc(sem("wo_in"), 16)
                if not gated:
                    sp.dma_start(bi[:], io[b_in]).then_inc(sem("bi_in"), 16)
                    sp.dma_start(bo[:], io[b_out]).then_inc(sem("bi_in"), 16)
                sp.wait_ge(sem("zeros_ready"), 1)
                for e in range(E):
                    sp.dma_start(io[src][SPARE + e * P:SPARE + (e + 1) * P, :], zeros[:]).then_inc(sem("spare_out"), 16)
                sp.wait_ge(sem("plan_ready"), 2)
                sp.wait_ge(sem("pad_out"), 16 * E)
                sp.wait_ge(sem("spare_out"), 16 * E)

                def step(s, on):
                    if on[0]:
                        r = which(sp, row, s, ROWS - P)
                        need(sp, sem("xT_ready"), s.b - 3)
                        sp.dma_start(x[s.par][:], io[src][bass.ds(r, P), :]).then_inc(sem(f"x_in{s.par}"), 16)

                loop(sp, step)

            @block.gpsimd
            def _(pool):
                nc.gpsimd.memset(ones8[:], 1.0).then_inc(sem("ones8_ready"), 1)
                nc.gpsimd.memset(zeros[:], 0.0).then_inc(sem("zeros_ready"), 1)
                pool.wait_ge(sem("zeros_ready"), 1)
                pool.wait_ge(sem("pad_ready"), E)
                for e in range(E):
                    pool.indirect_dma_start(
                        out=io[src], out_offset=bass.IndirectOffsetOnAxis(ap=pad[e][:], axis=0),
                        in_=zeros[:], in_offset=None).then_inc(sem("pad_out"), 16)

                def step(s, on):
                    if on[3]:
                        b = s.back(3)
                        pool.wait_ge(sem("y_ready"), b.b + 1)
                        pool.dma_start(io[dst][bass.ds(P * b.b, P), :], y[b.par][:]).then_inc(sem(f"y_out{b.par}"), 16)

                loop(pool, step)
                for k in range(4):
                    pool.wait_ge(sem(f"y_out{k}"), 16 * BLOCKS // 4)

            @block.vector
            def _(dve):
                v = nc.vector
                own = Own(dve, sem("own"), sem("dve_passed"))
                dve.wait_ge(sem("lane_in"), 32)
                dve.wait_ge(sem("ones8_ready"), 1)
                own.did(v.tensor_scalar(padf[:], keep.run[:], lane[:, 0:1], None, ALU.add))
                own.did(v.tensor_scalar(offs[:], keep.iota[:], float(REGION), None, ALU.mult))
                own.wait()
                for e in range(E):
                    v.tensor_copy(pad[e][:], padf[:, e:e + 1]).then_inc(sem("pad_ready"), 1)
                own.did(v.tensor_tensor(count[:], keep.run[:], offs[:], ALU.subtract))
                own.wait()
                own.did(v.tensor_scalar(blocks[:], count[:], P - 1.0, 1.0 / P, ALU.add, ALU.mult))
                own.wait()
                own.did(v.tensor_scalar(blocks[:], blocks[:], 0.5 / P - 0.5, None, ALU.add))
                own.wait()
                own.did(v.tensor_scalar(blocks[:], blocks[:], ROUND, ROUND, ALU.add, ALU.subtract))
                own.wait()
                own.did(v.tensor_tensor_scan(ends[:], ones8[:], blocks[:], 0.0, ALU.mult, ALU.add))
                own.wait()
                many = [P, BLOCKS, E]
                own.did(v.tensor_tensor(past[:], turn[:].unsqueeze(2).to_broadcast(many),
                                        ends[:].unsqueeze(1).to_broadcast(many), ALU.is_ge))
                own.wait()
                own.did(v.tensor_reduce(ef[:], past[:], AX, ALU.add))
                own.did(v.tensor_tensor(count[:], ends[:], blocks[:], ALU.subtract))
                own.wait()
                v.tensor_scalar(expert[:], ef[:], E - 1.0, None, ALU.min).then_inc(sem("plan_ready"), 1)
                own.did(v.tensor_tensor(isf[:], keep.iota[:].unsqueeze(1).to_broadcast(many),
                                        ef[:].unsqueeze(2).to_broadcast(many), ALU.is_equal))
                own.did(v.scalar_tensor_tensor(offs[:], count[:], -float(P), offs[:], ALU.mult, ALU.add))
                own.did(v.tensor_scalar(spare[:], ef[:], E - 0.5, None, ALU.is_ge))
                own.did(v.tensor_scalar(rowf[:], turn[:], float(P), None, ALU.mult))
                own.wait()
                own.did(v.scalar_tensor_tensor(spare[:], rowf[:], float(SPARE - NB * N), spare[:], ALU.add, ALU.mult))
                own.did(v.tensor_tensor(past[:], offs[:].unsqueeze(1).to_broadcast(many),
                                        rowf[:].unsqueeze(2).to_broadcast(many), ALU.add))
                own.wait()
                own.did(v.tensor_tensor(past[:], past[:], isf[:], ALU.mult))
                own.wait()
                own.did(v.tensor_reduce(rowf[:], past[:], AX, ALU.add))
                own.wait()
                v.tensor_tensor(row[:], rowf[:], spare[:], ALU.add).then_inc(sem("plan_ready"), 1)
                dve.wait_ge(sem("plan_ready"), 2)
                pairs = [P, NB * T, E]
                slots = keep.slots[:].unsqueeze(2).to_broadcast(pairs)
                at_least, its = past[:, 0:NB * T, :], isf[:, 0:NB * T, :]
                own.did(v.tensor_scalar(padf[:], keep.iota[:], float(REGION), None, ALU.mult))
                own.wait()
                own.did(v.tensor_tensor(at_least, slots, padf[:].unsqueeze(1).to_broadcast(pairs), ALU.is_ge))
                own.wait()
                own.did(v.tensor_reduce(chosen[:], at_least, AX, ALU.add))
                own.wait()
                own.did(v.tensor_scalar(chosen[:], chosen[:], -1.0, None, ALU.add))
                own.wait()
                own.did(v.tensor_tensor(its, chosen[:].unsqueeze(2).to_broadcast(pairs),
                                        keep.iota[:].unsqueeze(1).to_broadcast(pairs), ALU.is_equal))
                own.wait()
                own.did(v.tensor_tensor(its, its, offs[:].unsqueeze(1).to_broadcast(pairs), ALU.mult))
                own.wait()
                own.did(v.tensor_reduce(chosen[:], its, AX, ALU.add))
                own.wait()
                v.tensor_tensor(keep.rows[:], keep.slots[:], chosen[:], ALU.subtract)
                if not gated:
                    dve.wait_ge(sem("bi_in"), 32)

                def step(s, on):
                    if on[1]:
                        b = s.back()
                        e = None if gated else which(dve, expert, b, E - 1)
                        dve.wait_ge(sem("h_ps"), b.b + 1)
                        need(dve, sem("hT_ps"), b.b - 1)
                        if gated:
                            dve.wait_ge(sem("gate_ready"), b.b + 1)
                            v.tensor_tensor(h[b.par % 2][:], h_ps[b.par % 2][:, FH:2 * FH], gate[b.par % 2][:], ALU.mult
                                            ).then_inc(sem("h_ready"), 1)
                        else:
                            v.tensor_tensor(h[b.par % 2][:], h_ps[b.par % 2][:, 0:FH],
                                            bi[:, bass.ds(e, 1), :].rearrange("p o f -> p (o f)"), ALU.add
                                            ).then_inc(sem("h_ready"), 1)
                    if on[3]:
                        b = s.back(3)
                        e = None if gated else which(dve, expert, b, E - 1)
                        dve.wait_ge(sem("y_ps"), b.b + 1)
                        need(dve, sem(f"y_out{b.par}"), 16 * b.half)
                        if gated:
                            v.tensor_copy(y[b.par][:], y_ps[b.par % 2][:, 0:W]).then_inc(sem("y_ready"), 1)
                        else:
                            v.tensor_tensor(y[b.par][:], y_ps[b.par % 2][:, 0:W],
                                            bo[:, bass.ds(e, 1), :].rearrange("p o f -> p (o f)"), ALU.add
                                            ).then_inc(sem("y_ready"), 1)

                loop(dve, step)

            @block.scalar
            def _(act):
                def step(s, on):
                    if on[0]:
                        act.wait_ge(sem("xT_ready"), s.b + 1)
                        need(act, sem("h_ps"), s.b - 1)
                        nc.scalar.copy(xT[s.par % 2][:], xT_ps[s.par % 2][:, 0:P]).then_inc(sem("xT_taken"), 1)
                    if on[1] and gated:
                        b = s.back()
                        act.wait_ge(sem("h_ps"), b.b + 1)
                        need(act, sem("h_ready"), b.b - 1)
                        nc.scalar.activation(gate[b.par % 2][:], h_ps[b.par % 2][:, 0:FH], ACT.Silu
                                             ).then_inc(sem("gate_ready"), 1)
                    if on[2]:
                        b = s.back(2)
                        act.wait_ge(sem("hT_ps"), b.b + 1)
                        need(act, sem("y_ps"), b.b - 1)
                        nc.scalar.activation(hT[b.par % 2][:], hT_ps[b.par % 2][:, 0:FH].rearrange("p (k n) -> p k n", k=2),
                                             ACT.Copy if gated else ACT.Relu).then_inc(sem("hT_ready"), 1)

                loop(act, step)

            @block.tensor
            def _(pe):
                pe.wait_ge(sem("plan_ready"), 2)
                pe.wait_ge(sem("wi_in"), 16)
                pe.wait_ge(sem("wo_in"), 16)

                def step(s, on):
                    if on[0]:
                        pe.wait_ge(sem(f"x_in{s.par}"), 16 * s.half + 16)
                        need(pe, sem("xT_taken"), s.b - 1)
                        nc.tensor.transpose(xT_ps[s.par % 2][:, 0:P], x[s.par][:], keep.ident[:]).then_inc(sem("xT_ready"), 1)
                    if on[1]:
                        b = s.back()
                        e = which(pe, expert, b, E - 1)
                        pe.wait_ge(sem("xT_taken"), b.b + 1)
                        need(pe, sem("h_ready"), b.b - 1)
                        nc.tensor.matmul(h_ps[b.par % 2][:, 0:wide], xT[b.par % 2][:],
                                         wi[:, bass.ds(e, 1), :].rearrange("p o f -> p (o f)"), start=True, stop=True
                                         ).then_inc(sem("h_ps"), 1)
                    if on[2]:
                        b = s.back(2)
                        pe.wait_ge(sem("h_ready"), b.b + 1)
                        need(pe, sem("hT_ready"), b.b - 1)
                        for k in range(2):
                            mm = nc.tensor.transpose(hT_ps[b.par % 2][:, k * P:(k + 1) * P], h[b.par % 2][:, k * P:(k + 1) * P],
                                                     keep.ident[:])
                        mm.then_inc(sem("hT_ps"), 1)
                    if on[3]:
                        b = s.back(3)
                        e = which(pe, expert, b, E - 1)
                        pe.wait_ge(sem("hT_ready"), b.b + 1)
                        need(pe, sem("y_ready"), b.b - 1)
                        for k in range(2):
                            mm = nc.tensor.matmul(y_ps[b.par % 2][:, 0:W], hT[b.par % 2][:, k, :],
                                                  wo[:, bass.ds(e, 1), k, :].rearrange("p o f -> p (o f)"),
                                                  start=(k == 0), stop=(k == 1))
                        mm.then_inc(sem("y_ps"), 1)

                loop(pe, step)


def attention_two(nc, g, keep):
    io = g.io
    G = 4
    GROUPS = H // G
    PARTS = 3
    ROWS_QK = PARTS * PARTS * HD
    ROWS_ALL = ROWS_QK + PARTS
    VC = 32
    PAIRS = 2 * T

    def sem(name):
        return g.sem(f"c_{name}")

    with ExitStack() as ctx:
        def sb(name, shape, dt=F32):
            return ctx.enter_context(nc.sbuf_tensor(f"c_{name}", shape, dt))

        s_ps = [ctx.enter_context(nc.psum_tensor(f"c_s{i}", [P, 2, N], F32)) for i in range(2)]
        m_ps = [ctx.enter_context(nc.psum_tensor(f"c_m{i}", [P, N], F32)) for i in range(2)]
        o_ps = ctx.enter_context(nc.psum_tensor("c_o", [P, N], F32))
        misc = ctx.enter_context(nc.psum_tensor("c_misc", [P, N], F32))
        tiles = misc[:].rearrange("p (t w) -> p t w", t=T)
        mT_ps = misc[:].bitcast(BF16)[0:PARTS * G * T, 0:P]
        rl_ps = misc[:, 0:T * E].rearrange("p (t e) -> p t e", t=T)
        before_ps = misc[:, 64:64 + T * E].rearrange("p (t e) -> p t e", t=T)
        total_ps = misc[:, 128:128 + T * E].rearrange("p (t e) -> p t e", t=T)

        wq, wk, wv, wout = (sb(n, [P, W]) for n in ("wq", "wkk", "wvv", "wout"))
        gw = sb("gw", [P, E])
        identb = sb("identb", [P, P], BF16)
        x1 = [sb(f"x1{i}", [P, T, W]) for i in range(2)]
        yb = [sb(f"yb{i}", [P, T, W]) for i in range(2)]
        rows = [sb(f"rows{i}", [P, T], U32) for i in range(2)]
        xr = sb("xr", [P, T, W])
        st = sb("st", [P, T, 6])
        mv = sb("mv", [P, T, 2])
        ve = sb("ve", [P, T])
        rstd = sb("rstd", [P, T])
        x2 = [sb(f"x2{i}", [P, T, W]) for i in range(2)]
        res = sb("res", [P, T, W])
        xT = sb("xT", [P, T, P])
        xT3 = sb("xT3", [P, T, P])
        qk = sb("qk", [P, 2, N])
        rest = sb("rest", [P, N])
        parts = sb("parts", [P, 2, PARTS, N], BF16)
        qst = [sb(f"qst{i}", [ROWS_ALL, H, N], BF16) for i in range(2)]
        kst = [sb(f"kst{i}", [ROWS_ALL, H, N], BF16) for i in range(2)]
        vst = [sb(f"vst{i}", [P, T, H, VC]) for i in range(2)]
        junk = [sb(f"junk{i}", [P, N], BF16) for i in range(2)]
        mx = sb("mx", [P, G * T])
        mrest = sb("mrest", [P, G * T])
        mparts = sb("mparts", [P, PARTS, G * T], BF16)
        mT = [sb(f"mT{i}", [PARTS * G * T, P], BF16) for i in range(2)]
        prob = [sb(f"prob{i}", [P, G, N]) for i in range(2)]
        oT = sb("oT", [P, N])
        rden = sb("rden", [P, T, G])
        att = [sb(f"att{i}", [P, T, H, HD]) for i in range(2)]
        x3 = [sb(f"x3{i}", [P, T, W]) for i in range(2)]
        xs = [sb(f"xs{i}", [P, T, W]) for i in range(2)]
        lg = sb("lg", [P, T, E])
        top = sb("top", [P, T, 8])
        idx = sb("idx", [P, T, 8], U32)
        idxf = sb("idxf", [P, T])
        oh = sb("oh", [P, T, E])
        runs = sb("runs", [P, T, E])
        sel = sb("sel", [P, T, E])
        slotf = sb("slotf", [P, T])
        slot = [sb(f"slot{i}", [P, T], U32) for i in range(2)]
        sig = sb("sig", [P, T])
        score = sb("score", [P, T])

        def ahead(s, j):
            return (s, j + 2) if j < 2 else (s.ahead(), j - 2)

        def bodies(eng, body, own=None, per=0):
            body(at(0), tail=False)
            with eng.Fori(0, NB // 2 - 1) as i:
                if own:
                    own.enter(i, per)
                for s in steps(i, 2):
                    body(s.back())
            if own:
                own.leave(NB // 2 - 1)
            body(at(NB - 1), front=False)

        with nc.Block() as block:

            @block.sync
            def _(sp):
                for d, name in ((wq, "wq"), (wk, "wkk"), (wv, "wvv"), (wout, "wout"), (gw, "gw")):
                    sp.dma_start(d[:], io[name]).then_inc(sem("w_in"), 16)

                def load(s):
                    need(sp, sem("x2_ready"), s.b - 1)
                    sp.dma_start(x1[s.par][:], io["x1_d"][bass.ds(s.b, 1)].rearrange("o p t w -> p (o t) w")
                                 ).then_inc(sem(f"x1_in{s.par}"), 16)

                def stack(s):
                    sp.wait_ge(sem("parts_ready"), 2 * s.b + 2)
                    for w in range(2):
                        sp.dma_start(io["parts_d"][s.par, w].rearrange("a p n -> p a n"), parts[:, w]
                                     ).then_inc(sem(f"parts_out{s.par}"), 16)
                    sp.wait_ge(sem(f"parts_out{s.par}"), 32 * s.half + 32)
                    apart(sp, sem("sp_passed"))
                    need(sp, sem("s_ready"), H * T // 2 * (s.b - 1))
                    for a in range(PARTS):
                        r0 = a * PARTS * HD
                        sp.dma_start(kst[s.par][r0:r0 + PARTS * HD], io["parts_d"][s.par, 1].rearrange(
                            "a (d h) n -> (a d) h n", h=H)).then_inc(sem(f"stack_in{s.par}"), 16)
                        for c in range(PARTS):
                            sp.dma_start(qst[s.par][r0 + c * HD:r0 + (c + 1) * HD], io["parts_d"][s.par, 0, a].rearrange(
                                "(d h) n -> d h n", h=H)).then_inc(sem(f"stack_in{s.par}"), 16)

                def max_rows(s, j):
                    sp.wait_ge(sem("mT_ready"), GROUPS * s.b + j + 1)
                    for a in range(PARTS):
                        dst = qst[s.par][ROWS_QK + a:ROWS_QK + a + 1, G * j:G * j + G, :]
                        sp.dma_start(dst.rearrange("o h (t p) -> o (h t) p", p=P), mT[j % 2][a * G * T:(a + 1) * G * T, :]
                                     ).then_inc(sem(f"max_in{j}"), 16)

                def store(s):
                    sp.wait_ge(sem("x3_ready"), s.b + 1)
                    sp.dma_start(io["x3_d"][bass.ds(s.b, 1)].rearrange("o p t w -> p (o t) w"), x3[s.par][:]
                                 ).then_inc(sem(f"x3_out{s.par}"), 16)

                def body(s, tail=True, front=True):
                    max_rows(s, 1)
                    max_rows(s, 2)
                    if front:
                        stack(s.ahead())
                    max_rows(s, 3)
                    if tail:
                        store(s.back())
                    if front:
                        max_rows(s.ahead(), 0)

                load(at(0))
                load(at(1))
                sp.wait_ge(sem("kst_ones"), 2)
                stack(at(0))
                max_rows(at(0), 0)

                def body_and_load(s, tail=True, front=True):
                    body(s, tail, front)
                    if not isinstance(s.b, int) or s.b + 2 < NB:
                        load(s.ahead().ahead())

                body_and_load(at(0), tail=False)
                with sp.Fori(0, NB // 2 - 2) as i:
                    for s in steps(i, 2):
                        body_and_load(s.back())
                body_and_load(at(NB - 3))
                body_and_load(at(NB - 2))
                body_and_load(at(NB - 1), front=False)
                store(at(NB - 1))
                for k in range(2):
                    sp.wait_ge(sem(f"x3_out{k}"), 16 * NB // 2)

            @block.gpsimd
            def _(pool):
                for k in range(2):
                    nc.gpsimd.memset(vst[k][:], 0.0).then_inc(sem("vst_zero"), 1)
                    pool.wait_ge(sem("vst_zero"), k + 1)
                    nc.gpsimd.memset(vst[k][:, :, :, HD:HD + 1], 1.0).then_inc(sem("vst_ones"), 1)
                    pool.wait_ge(sem("vst_ones"), k + 1)

                def gather(s):
                    need(pool, sem("x2_ready"), s.b - 1)
                    need(pool, sem(f"y_in{s.par}"), 16 * T * s.half)
                    apart(pool, sem("pool_passed"))
                    nc.gpsimd.tensor_copy(rows[s.par][:], keep.rows[:, bass.ds(T * s.b, T)]).then_inc(sem("rows_ready"), 1)
                    pool.wait_ge(sem("rows_ready"), s.b + 1)
                    apart(pool, sem("pool_passed"))
                    for t in range(T):
                        pool.indirect_dma_start(
                            out=yb[s.par][:, t, :], out_offset=None, in_=io["ys_d"],
                            in_offset=bass.IndirectOffsetOnAxis(ap=rows[s.par][:, t:t + 1], axis=0)
                        ).then_inc(sem(f"y_in{s.par}"), 16)

                def power(n):
                    pool.wait_ge(sem("var_ready"), n)
                    nc.gpsimd.tensor_tensor(rstd[:], ve[:], keep.minus_half[:], ALU.pow).then_inc(sem("rstd_ready"), 1)

                def split(s):
                    for w in range(2):
                        pool.wait_ge(sem("qk_taken"), 2 * s.b + w + 1)
                        if w == 0:
                            need(pool, sem(f"parts_out{1 - s.par}"), 32 * (s.half + s.par))
                        for a in range(PARTS - 1):
                            src = qk[:, w] if a == 0 else rest[:]
                            apart(pool, sem("pool_passed"))
                            ops.did(nc.gpsimd.tensor_copy(parts[:, w, a], src))
                            ops.wait()
                            dst = rest[:] if a == 0 else parts[:, w, 2]
                            ins = nc.gpsimd.tensor_tensor(dst, src, parts[:, w, a], ALU.subtract)
                            if a == 0:
                                ops.did(ins)
                                ops.wait()
                            else:
                                ins.then_inc(sem("parts_ready"), 1)
                                pool.wait_ge(sem("parts_ready"), 2 * s.b + w + 1)

                def scatter(s):
                    pool.wait_ge(sem("slot_ready"), s.b + 1)
                    apart(pool, sem("pool_passed"))
                    for t in range(T):
                        pool.indirect_dma_start(
                            out=io["zs_d"], out_offset=bass.IndirectOffsetOnAxis(ap=slot[s.par][:, t:t + 1], axis=0),
                            in_=xs[s.par][:, t, :], in_offset=None).then_inc(sem(f"scat{s.par}"), 16)

                def body(s, tail=True, front=True):
                    if front:
                        power(2 * s.b + 1 if tail else 2)
                        split(s.ahead())
                        if not isinstance(s.b, int) or s.b + 3 < NB:
                            gather(s.ahead().ahead().ahead())
                    if tail:
                        power(2 * s.b + 2 if front else 2 * NB - 1)
                        scatter(s.back())

                ops = Own(pool, sem("pool_own"))
                gather(at(0))
                gather(at(1))
                power(1)
                split(at(0))
                gather(at(2))
                body(at(0), tail=False)
                with pool.Fori(0, NB // 2 - 2) as i:
                    ops.enter(i, C_POOL)
                    for s in steps(i, 2):
                        body(s.back())
                ops.leave(NB // 2 - 2)
                body(at(NB - 3))
                body(at(NB - 2))
                body(at(NB - 1), front=False)
                power(2 * NB)
                scatter(at(NB - 1))
                for k in range(2):
                    pool.wait_ge(sem(f"scat{k}"), 16 * T * NB // 2)

            @block.tensor
            def _(pe):
                def max_tile(s, j, n):
                    k = GROUPS * G * T * s.b + j * G * T + n
                    if n == 0:
                        pe.wait_ge(sem(f"stack_in{s.par}"), 192 * s.half + 192)
                    need(pe, sem("mx_read"), k - 1)
                    h, t = G * j + n // T, n % T
                    nc.tensor.matmul(m_ps[n % 2][:], qst[s.par][0:ROWS_QK, h, t * P:(t + 1) * P], kst[s.par][0:ROWS_QK, h, :],
                                     start=True, stop=True).then_inc(sem("mx_ps"), 1)

                def max_turn(s, j):
                    pe.wait_ge(sem("mparts_ready"), GROUPS * s.b + j + 1)
                    apart(pe, sem("pe_passed"))
                    nc.tensor.transpose(mT_ps, mparts[:].rearrange("p a n -> p (a n)"), identb[:]).then_inc(sem("mT_ps"), 1)

                def scores(s, j, n):
                    k = GROUPS * PAIRS * s.b + PAIRS * j + n
                    if n == 0:
                        pe.wait_ge(sem(f"max_in{j}"), 48 * s.b + 48)
                    need(pe, sem("exp_done"), k - 1)
                    tj = n // 2
                    for i in range(2):
                        h = G * j + 2 * (n % 2) + i
                        nc.tensor.matmul(s_ps[n % 2][:, i, :], kst[s.par][:, h, tj * P:(tj + 1) * P], qst[s.par][:, h, :],
                                         start=True, stop=False, skip_group_check=True)
                        for ti in range(T):
                            mm = nc.tensor.matmul(s_ps[n % 2][:, i, ti * P:(ti + 1) * P], keep.bias[:, h, T - 1 + tj - ti, :],
                                                  keep.ident[:], is_transpose=True, start=False, stop=True, skip_group_check=True)
                    mm.then_inc(sem("s_ready"), 1)

                def values(s, j, tj):
                    pe.wait_ge(sem("exp_done"), GROUPS * PAIRS * s.b + PAIRS * j + 2 * tj + 2)
                    if tj == 0:
                        need(pe, sem("o_taken"), GROUPS * s.b + j)
                    for i in range(G):
                        mm = nc.tensor.matmul(o_ps[VC * i:VC * i + VC, :], vst[s.par][:, tj, G * j + i, :], prob[tj % 2][:, i, :],
                                              start=(tj == 0), stop=(tj == T - 1))
                    mm.then_inc(sem("pv_done"), 1)

                def out_turn(s, j):
                    pe.wait_ge(sem("o_taken"), GROUPS * s.b + j + 1)
                    for t in range(T):
                        mm = nc.tensor.transpose(tiles[:, t, :], oT[:, t * P:(t + 1) * P], keep.ident[:])
                    mm.then_inc(sem("on_ps"), 1)

                def front_turn(s):
                    pe.wait_ge(sem("x2_ready"), s.b + 1)
                    for t in range(T):
                        mm = nc.tensor.transpose(tiles[:, t, :], x2[s.par][:, t, :], keep.ident[:])
                    mm.then_inc(sem("x2T_ps"), 1)

                def front_qk(s, w):
                    pe.wait_ge(sem("x2T_ready"), s.b + 1)
                    if w == 1:
                        pe.wait_ge(sem("qk_taken"), 2 * s.b + 1)
                    nc.tensor.matmul(misc[:], (wq, wk)[w][:], xT[:].rearrange("p t n -> p (t n)"), start=True, stop=True
                                     ).then_inc(sem("qk_ps"), 1)

                def front_v(s):
                    pe.wait_ge(sem("qk_taken"), 2 * s.b + 2)
                    for t in range(T):
                        mm = nc.tensor.matmul(tiles[:, t, :], xT[:, t, :], wv[:], start=True, stop=True)
                    mm.then_inc(sem("v_ps"), 1)

                def tail_turn(s):
                    pe.wait_ge(sem("on_read"), GROUPS * s.b + GROUPS)
                    for t in range(T):
                        mm = nc.tensor.transpose(tiles[:, t, :], att[s.par][:, t].rearrange("p h d -> p (h d)"), keep.ident[:])
                    mm.then_inc(sem("attT_ps"), 1)

                def tail_out(s):
                    pe.wait_ge(sem("attT_ready"), s.b + 1)
                    for t in range(T):
                        mm = nc.tensor.matmul(tiles[:, t, :], xT3[:, t, :], wout[:], start=True, stop=True)
                    mm.then_inc(sem("y_ps"), 1)

                def route_turn(s):
                    pe.wait_ge(sem("x3_ready"), s.b + 1)
                    for t in range(T):
                        mm = nc.tensor.transpose(tiles[:, t, :], x3[s.par][:, t, :], keep.ident[:])
                    mm.then_inc(sem("x3T_ps"), 1)

                def route_logits(s):
                    pe.wait_ge(sem("x3T_ready"), s.b + 1)
                    for t in range(T):
                        mm = nc.tensor.matmul(rl_ps[:, t, :], xT3[:, t, :], gw[:], start=True, stop=True)
                    mm.then_inc(sem("rl_ps"), 1)

                def route_count(s):
                    pe.wait_ge(sem("oh_ready"), s.b + 1)
                    nc.tensor.matmul(before_ps, keep.tri[:], oh[:], start=True, stop=True)
                    nc.tensor.matmul(total_ps, keep.ones[:], oh[:], start=True, stop=True).then_inc(sem("count_ready"), 1)

                def body(s, tail=True, front=True):
                    for j in range(GROUPS):
                        sm, jm = ahead(s, j)
                        for n in range(PAIRS):
                            scores(s, j, n)
                            if j < 2 or front:
                                max_tile(sm, jm, 2 * n)
                                max_tile(sm, jm, 2 * n + 1)
                            last = GROUPS * s.b + j
                            if n == 0 and (j < 3 or front):
                                if j == 0:
                                    if tail:
                                        pe.wait_ge(sem("on_read"), last - 1)
                                    max_turn(s, 1)
                                elif j == 1:
                                    if front:
                                        pe.wait_ge(sem("v_taken"), s.b + 2)
                                    else:
                                        pe.wait_ge(sem("on_read"), GROUPS * s.b)
                                    max_turn(s, 2)
                                elif j == 2:
                                    if tail:
                                        pe.wait_ge(sem("y_read"), s.b)
                                    else:
                                        pe.wait_ge(sem("on_read"), last - 1)
                                    max_turn(s, 3)
                                else:
                                    pe.wait_ge(sem("count_read"), s.b) if tail else pe.wait_ge(sem("on_read"), last - 1)
                                    max_turn(s.ahead(), 0)
                            if n == 1 and (j > 0 or tail):
                                values(*((s, j - 1) if j else (s.back(), GROUPS - 1)), T - 1)
                            if n == 2 and (j > 0 or tail):
                                if j < 3 or front:
                                    pe.wait_ge(sem("mT_ready"), last + 2)
                                else:
                                    pe.wait_ge(sem("count_read"), s.b)
                                out_turn(*((s, j - 1) if j else (s.back(), GROUPS - 1)))
                            if j == 0 and front:
                                if n == 3:
                                    if tail:
                                        pe.wait_ge(sem("on_read"), GROUPS * s.b)
                                    else:
                                        pe.wait_ge(sem("mT_ready"), 2)
                                    front_turn(s.ahead())
                                if n == 4:
                                    front_qk(s.ahead(), 0)
                                if n == 5:
                                    front_qk(s.ahead(), 1)
                                if n == 6:
                                    front_v(s.ahead())
                            if j == 1 and tail:
                                if n == 3:
                                    pe.wait_ge(sem("on_read"), last)
                                    tail_turn(s.back())
                                if n == 4:
                                    tail_out(s.back())
                            if j == 2 and tail:
                                if n == 3:
                                    pe.wait_ge(sem("on_read"), last)
                                    route_turn(s.back())
                                if n == 4:
                                    route_logits(s.back())
                                if n == 6:
                                    route_count(s.back())
                            if n % 2 == 1 and n >= 3:
                                values(s, j, n // 2 - 1)

                pe.wait_ge(sem("w_in"), 80)
                pe.wait_ge(sem("identb_ready"), 1)
                front_turn(at(0))
                front_qk(at(0), 0)
                front_qk(at(0), 1)
                front_v(at(0))
                pe.wait_ge(sem("v_taken"), 1)
                pe.wait_ge(sem("kst_ones"), 2)
                pe.wait_ge(sem("vst_ones"), 2)
                for n in range(G * T):
                    max_tile(at(0), 0, n)
                max_turn(at(0), 0)
                for n in range(G * T):
                    max_tile(at(0), 1, n)
                pe.wait_ge(sem("mT_ready"), 1)
                bodies(pe, body)
                s = at(NB - 1)
                values(s, GROUPS - 1, T - 1)
                pe.wait_ge(sem("on_read"), GROUPS * NB - 1)
                out_turn(s, GROUPS - 1)
                tail_turn(s)
                tail_out(s)
                pe.wait_ge(sem("y_read"), NB)
                route_turn(s)
                route_logits(s)
                route_count(s)

            @block.scalar
            def _(act):
                def exps(s, j, n):
                    act.wait_ge(sem("s_ready"), GROUPS * PAIRS * s.b + PAIRS * j + n + 1)
                    need(act, sem("pv_done"), GROUPS * T * s.b + T * j + n // 2 - 1)
                    i = 2 * (n % 2)
                    nc.scalar.activation(prob[n // 2 % 2][:, i:i + 2, :], s_ps[n % 2][:], ACT.Exp).then_inc(sem("exp_done"), 1)

                def max_copy(s, j):
                    act.wait_ge(sem("mT_ps"), GROUPS * s.b + j + 1)
                    if isinstance(s.b, int) and s.b == 0:
                        if j >= 2:
                            act.wait_ge(sem(f"max_in{j - 2}"), 48)
                    elif j >= 2:
                        act.wait_ge(sem(f"max_in{j - 2}"), 48 * s.b + 48)
                    else:
                        act.wait_ge(sem(f"max_in{j + 2}"), 48 * s.b)
                    nc.scalar.copy(mT[j % 2][:], mT_ps).then_inc(sem("mT_ready"), 1)

                def out_copy(s, j):
                    act.wait_ge(sem("pv_done"), GROUPS * T * s.b + T * j + T)
                    need(act, sem("on_ps"), GROUPS * s.b + j)
                    nc.scalar.copy(oT[:], o_ps[:]).then_inc(sem("o_taken"), 1)

                def front_turn(s):
                    act.wait_ge(sem("x2T_ps"), s.b + 1)
                    need(act, sem("v_ps"), s.b)
                    nc.scalar.copy(xT[:], tiles).then_inc(sem("x2T_ready"), 1)

                def front_qk(s, w):
                    act.wait_ge(sem("qk_ps"), 2 * s.b + w + 1)
                    need(act, sem("parts_ready"), 2 * s.b + w - 1)
                    nc.scalar.activation(qk[:, w], misc[:], ACT.Copy, scale=HD ** -0.5 if w == 0 else 1.0
                                         ).then_inc(sem("qk_taken"), 1)

                def front_v(s):
                    act.wait_ge(sem("v_ps"), s.b + 1)
                    need(act, sem("pv_done"), GROUPS * T * (s.b - 1))
                    for t in range(T):
                        ins = nc.scalar.copy(vst[s.par][:, t, :, 0:HD], tiles[:, t, :].rearrange("p (h d) -> p h d", h=H))
                    ins.then_inc(sem("v_taken"), 1)

                def tail_turn(s):
                    act.wait_ge(sem("attT_ps"), s.b + 1)
                    need(act, sem("rl_ps"), s.b)
                    nc.scalar.copy(xT3[:], tiles).then_inc(sem("attT_ready"), 1)

                def route_turn(s):
                    act.wait_ge(sem("x3T_ps"), s.b + 1)
                    nc.scalar.copy(xT3[:], tiles).then_inc(sem("x3T_ready"), 1)

                def route_exp(s):
                    act.wait_ge(sem("oh_ready"), s.b + 1)
                    need(act, sem("xs_ready"), s.b)
                    nc.scalar.activation(sig[:], top[:, :, 0], ACT.Exp, scale=-1.0).then_inc(sem("sig_ready"), 1)

                def body(s, tail=True, front=True):
                    for j in range(GROUPS):
                        for n in range(PAIRS):
                            exps(s, j, n)
                            if n == 0 and (j < 3 or front):
                                max_copy(*((s, j + 1) if j < 3 else (s.ahead(), 0)))
                            if n == 1 and (j > 0 or tail):
                                out_copy(*((s, j - 1) if j else (s.back(), GROUPS - 1)))
                            if j == 0 and front:
                                if n == 3:
                                    front_turn(s.ahead())
                                if n in (4, 5):
                                    front_qk(s.ahead(), n - 4)
                                if n == 6:
                                    front_v(s.ahead())
                            if j == 1 and tail and n == 3:
                                tail_turn(s.back())
                            if j == 2 and tail and n == 3:
                                route_turn(s.back())
                            if j == 2 and tail and n == 6:
                                route_exp(s.back())

                front_turn(at(0))
                front_qk(at(0), 0)
                front_qk(at(0), 1)
                act.wait_ge(sem("vst_ones"), 2)
                front_v(at(0))
                max_copy(at(0), 0)
                bodies(act, body)
                s = at(NB - 1)
                out_copy(s, GROUPS - 1)
                tail_turn(s)
                route_turn(s)
                route_exp(s)

            @block.vector
            def _(dve):
                v = nc.vector
                own = Own(dve, sem("own"), sem("dve_passed"))
                v.tensor_copy(identb[:], keep.ident[:]).then_inc(sem("identb_ready"), 1)
                own.did(v.tensor_scalar(keep.run[:], keep.iota[:], float(REGION), None, ALU.mult))
                own.wait()

                def front_norm(s, n):
                    dve.wait_ge(sem(f"x1_in{s.par}"), 16 * s.half + 16)
                    dve.wait_ge(sem(f"y_in{s.par}"), 16 * T * s.half + 16 * T)
                    own.did(v.tensor_tensor(yb[s.par][:], yb[s.par][:], keep.prob[:, bass.ds(T * s.b, T)].unsqueeze(2)
                                            .to_broadcast([P, T, W]), ALU.mult))
                    own.wait()
                    own.did(v.tensor_tensor(xr[:], yb[s.par][:], x1[s.par][:], ALU.add))
                    own.wait()
                    layer_norm(v, own, xr, x2[s.par], st, mv, ve, sem("var_ready"), sem("rstd_ready"), rstd, n, sem("x2_ready"))

                def max_tile(s, j, n):
                    k = GROUPS * G * T * s.b + j * G * T + n
                    if n == 0:
                        need(dve, sem("mparts_ready"), GROUPS * s.b + j)
                    need(dve, sem("mx_read"), k - 1)
                    dve.wait_ge(sem("mx_ps"), k + 1)
                    apart(dve, sem("dve_passed"))
                    h, t = G * j + n // T, n % T
                    bias = keep.bias[:, h, T - 1 - t:DELTA - t, :].rearrange("p t q -> p (t q)")
                    v.tensor_tensor_reduce(junk[n % 2][:], m_ps[n % 2][:], bias, 1.0, -3.0e38, ALU.add, ALU.max, mx[:, n:n + 1]
                                           ).then_inc(sem("mx_read"), 1)

                def max_parts(s, j):
                    dve.wait_ge(sem("mx_read"), GROUPS * G * T * s.b + (j + 1) * G * T)
                    need(dve, sem("mT_ps"), GROUPS * s.b + j)
                    own.did(v.tensor_scalar(mparts[:, 0], mx[:], -1.0, None, ALU.mult))
                    own.wait()
                    own.did(v.scalar_tensor_tensor(mrest[:], mx[:], -1.0, mparts[:, 0], ALU.mult, ALU.subtract))
                    own.wait()
                    own.did(v.tensor_copy(mparts[:, 1], mrest[:]))
                    own.wait()
                    v.tensor_tensor(mparts[:, 2], mrest[:], mparts[:, 1], ALU.subtract).then_inc(sem("mparts_ready"), 1)

                def out_norm(s, j):
                    dve.wait_ge(sem("on_ps"), GROUPS * s.b + j + 1)
                    if j == 0:
                        need(dve, sem("attT_ps"), s.b - 1)
                    heads = tiles.rearrange("p t (h c) -> p t h c", c=VC)
                    own.did(v.reciprocal(rden[:], heads[:, :, :, HD]))
                    own.wait()
                    v.tensor_tensor(att[s.par][:, :, G * j:G * j + G, :], heads[:, :, :, 0:HD],
                                    rden[:].unsqueeze(3).to_broadcast([P, T, G, HD]), ALU.mult).then_inc(sem("on_read"), 1)

                def tail_norm(s, n):
                    dve.wait_ge(sem("y_ps"), s.b + 1)
                    own.wait()
                    v.tensor_tensor(xr[:], tiles, res[:], ALU.add).then_inc(sem("y_read"), 1)
                    dve.wait_ge(sem("y_read"), s.b + 1)
                    need(dve, sem(f"x3_out{s.par}"), 16 * s.half)
                    layer_norm(v, own, xr, x3[s.par], st, mv, ve, sem("var_ready"), sem("rstd_ready"), rstd, n, sem("x3_ready"))

                def route_choose(s):
                    dve.wait_ge(sem("rl_ps"), s.b + 1)
                    own.did(v.tensor_copy(lg[:], rl_ps))
                    own.wait()
                    route(v, own, keep, lg, top, idx, idxf, oh)
                    v.tensor_tensor(oh[:], keep.iota[:].unsqueeze(1).to_broadcast([P, T, E]),
                                    idxf[:].unsqueeze(2).to_broadcast([P, T, E]), ALU.is_equal).then_inc(sem("oh_ready"), 1)

                def route_score(s):
                    dve.wait_ge(sem("sig_ready"), s.b + 1)
                    own.did(v.tensor_scalar(score[:], sig[:], 1.0, None, ALU.add))
                    own.wait()
                    own.did(v.reciprocal(score[:], score[:]))
                    own.wait()
                    need(dve, sem(f"scat{s.par}"), 16 * T * s.half)
                    dve.wait_ge(sem("x3_ready"), s.b + 1)
                    for t in range(T):
                        ins = v.tensor_scalar(xs[s.par][:, t, :], x3[s.par][:, t, :], score[:, t:t + 1], None, ALU.mult)
                    ins.then_inc(sem("xs_ready"), 1)

                def route_slots(s):
                    dve.wait_ge(sem("count_ready"), s.b + 1)
                    dve.wait_ge(sem("oh_ready"), s.b + 1)
                    slots_of(v, own, keep, runs, keep.run, oh, before_ps, total_ps, sel, slotf)
                    v.tensor_copy(keep.slots[:, bass.ds(T * s.b, T)], slotf[:]).then_inc(sem("count_read"), 1)
                    v.tensor_copy(slot[s.par][:], slotf[:]).then_inc(sem("slot_ready"), 1)

                def body(s, tail=True, front=True):
                    for j in range(GROUPS):
                        sm, jm = ahead(s, j)
                        if j == 0 and front:
                            front_norm(s.ahead(), 2 * s.b + 1 if tail else 2)
                        for n in range(PAIRS):
                            if j < 2 or front:
                                max_tile(sm, jm, 2 * n)
                                max_tile(sm, jm, 2 * n + 1)
                            if n == 2 and (j > 0 or tail):
                                out_norm(*((s, j - 1) if j else (s.back(), GROUPS - 1)))
                            if tail and j == 1 and n == 4:
                                tail_norm(s.back(), 2 * s.b + 2 if front else 2 * NB - 1)
                            if j == 2 and n == 0:
                                own.did(v.tensor_copy(res[:], x2[s.par][:]))
                            if tail and j == 2 and n == 5:
                                route_choose(s.back())
                            if tail and j == 2 and n == 7:
                                route_score(s.back())
                                route_slots(s.back())
                        if j < 2 or front:
                            max_parts(sm, jm)

                for k in range(2):
                    v.memset(kst[k][64:ROWS_ALL], 1.0).then_inc(sem("kst_ones"), 1)
                front_norm(at(0), 1)
                for j in range(2):
                    for n in range(G * T):
                        max_tile(at(0), j, n)
                    max_parts(at(0), j)
                bodies(dve, body, own, C_OWN)
                s = at(NB - 1)
                out_norm(s, GROUPS - 1)
                tail_norm(s, 2 * NB)
                route_choose(s)
                route_score(s)
                route_slots(s)


def finish(nc, g, keep):
    io = g.io
    CHUNKS = FH // P

    def sem(name):
        return g.sem(f"e_{name}")

    with ExitStack() as ctx:
        def sb(name, shape, dt=F32):
            return ctx.enter_context(nc.sbuf_tensor(f"e_{name}", shape, dt))

        bank = [ctx.enter_context(nc.psum_tensor(f"e_bank{i}", [P, N], F32)) for i in range(8)]
        turn_ps, gate_ps, up_ps = bank[0:2], bank[2:4], bank[4:6]
        y_ps = [b[:].rearrange("p (t w) -> p t w", t=T) for b in bank[6:8]]
        sgu = sb("sgu", [P, 2, FH])
        sd = sb("sd", [P, CHUNKS, W])
        x3 = [sb(f"x3{i}", [P, T, W]) for i in range(4)]
        rows = [sb(f"rows{i}", [P, T], U32) for i in range(4)]
        routed = [sb(f"routed{i}", [P, T, W]) for i in range(4)]
        xT = [sb(f"xT{i}", [P, N]) for i in range(2)]
        gate = [sb(f"gate{i}", [P, N]) for i in range(2)]
        h = [sb(f"h{i}", [P, CHUNKS, T, P]) for i in range(2)]
        part = sb("part", [P, T, W])
        xr = sb("xr", [P, T, W])
        st = sb("st", [P, T, 6])
        mv = sb("mv", [P, T, 2])
        ve = sb("ve", [P, T])
        rstd = sb("rstd", [P, T])
        y = [sb(f"y{i}", [P, T, W]) for i in range(4)]

        def loop(eng, step, own=None):
            for k in range(4):
                step(at(k, 4), [k >= n for n in range(3)])
            with eng.Fori(0, NB // 4 - 1) as i:
                if own:
                    own.enter(i, E_OWN)
                for s in steps(i, 4, 4):
                    step(s, [True] * 3)
            if own:
                own.leave(NB // 4 - 1)
            for k in range(NB, NB + 2):
                step(at(k, 4), [k - n < NB for n in range(3)])

        with nc.Block() as block:

            @block.sync
            def _(sp):
                sp.dma_start(sgu[:], io["sgu"]).then_inc(sem("w_in"), 16)
                sp.dma_start(sd[:], io["sd"]).then_inc(sem("w_in"), 16)

                def step(s, on):
                    if on[0]:
                        need(sp, sem("out_ready"), s.b - 3)
                        sp.dma_start(x3[s.par][:], io["x3_d"][bass.ds(s.b, 1)].rearrange("o p t w -> p (o t) w")
                                     ).then_inc(sem(f"x3_in{s.par}"), 16)
                    if on[2]:
                        b = s.back(2)
                        sp.wait_ge(sem("out_ready"), b.b + 1)
                        sp.dma_start(io["out"][bass.ds(b.b, 1)].rearrange("o p t w -> p (o t) w"), y[b.par][:]
                                     ).then_inc(sem(f"out{b.par}"), 16)

                loop(sp, step)
                for k in range(4):
                    sp.wait_ge(sem(f"out{k}"), 16 * NB // 4)

            @block.gpsimd
            def _(pool):
                def gather(s):
                    need(pool, sem("out_ready"), s.b - 3)
                    need(pool, sem(f"routed_in{s.par}"), 16 * T * s.half)
                    apart(pool, sem("pool_passed"))
                    nc.gpsimd.tensor_copy(rows[s.par][:], keep.rows[:, bass.ds(T * s.b, T)]).then_inc(sem("rows_ready"), 1)
                    pool.wait_ge(sem("rows_ready"), s.b + 1)
                    apart(pool, sem("pool_passed"))
                    for t in range(T):
                        pool.indirect_dma_start(
                            out=routed[s.par][:, t, :], out_offset=None, in_=io["us_d"],
                            in_offset=bass.IndirectOffsetOnAxis(ap=rows[s.par][:, t:t + 1], axis=0)
                        ).then_inc(sem(f"routed_in{s.par}"), 16)

                def step(s, on):
                    if on[0]:
                        gather(s)
                    if on[2]:
                        b = s.back(2)
                        pool.wait_ge(sem("var_ready"), b.b + 1)
                        nc.gpsimd.tensor_tensor(rstd[:], ve[:], keep.minus_half[:], ALU.pow).then_inc(sem("rstd_ready"), 1)

                loop(pool, step)

            @block.tensor
            def _(pe):
                def hidden(b, c):
                    need(pe, sem("h_ready"), CHUNKS * b.b + c - 1)
                    for k, ps in enumerate((gate_ps, up_ps)):
                        mm = nc.tensor.matmul(ps[c][:], sgu[:, k, c * P:(c + 1) * P], xT[b.par % 2][:], start=True, stop=True)
                    mm.then_inc(sem("hidden_ps"), 1)

                def step(s, on):
                    if on[0]:
                        pe.wait_ge(sem(f"x3_in{s.par}"), 16 * s.half + 16)
                        need(pe, sem("xT_ready"), s.b - 1)
                        for t in range(T):
                            mm = nc.tensor.transpose(turn_ps[s.par % 2][:, t * P:(t + 1) * P], x3[s.par][:, t, :], keep.ident[:])
                        mm.then_inc(sem("turn_ps"), 1)
                    if on[1]:
                        b = s.back()
                        pe.wait_ge(sem("xT_ready"), b.b + 1)
                        hidden(b, 0)
                    if on[2]:
                        b = s.back(2)
                        pe.wait_ge(sem("h_ready"), CHUNKS * b.b + CHUNKS)
                        need(pe, sem("y_read"), b.b - 1)
                        for t in range(T):
                            for c in range(CHUNKS):
                                mm = nc.tensor.matmul(y_ps[b.par % 2][:, t, :], h[b.par % 2][:, c, t, :], sd[:, c, :],
                                                      start=(c == 0), stop=(c == CHUNKS - 1))
                        mm.then_inc(sem("y_ps"), 1)
                    if on[1]:
                        hidden(s.back(), 1)

                pe.wait_ge(sem("w_in"), 32)
                loop(pe, step)

            @block.scalar
            def _(act):
                def step(s, on):
                    if on[0]:
                        act.wait_ge(sem("turn_ps"), s.b + 1)
                        need(act, sem("hidden_ps"), CHUNKS * (s.b - 1))
                        nc.scalar.copy(xT[s.par % 2][:], turn_ps[s.par % 2][:]).then_inc(sem("xT_ready"), 1)
                    if on[1]:
                        b = s.back()
                        for c in range(CHUNKS):
                            act.wait_ge(sem("hidden_ps"), CHUNKS * b.b + c + 1)
                            need(act, sem("h_ready"), CHUNKS * b.b + c - 1)
                            nc.scalar.activation(gate[c][:], gate_ps[c][:], ACT.Silu).then_inc(sem("gate_ready"), 1)

                loop(act, step)

            @block.vector
            def _(dve):
                v = nc.vector
                own = Own(dve, sem("own"), sem("dve_passed"))

                def step(s, on):
                    if on[1]:
                        b = s.back()
                        need(dve, sem("y_ps"), b.b - 1)
                        for c in range(CHUNKS):
                            dve.wait_ge(sem("gate_ready"), CHUNKS * b.b + c + 1)
                            v.tensor_tensor(h[b.par % 2][:, c].rearrange("p t n -> p (t n)"), up_ps[c][:], gate[c][:], ALU.mult
                                            ).then_inc(sem("h_ready"), 1)
                    if on[2]:
                        b = s.back(2)
                        dve.wait_ge(sem(f"x3_in{b.par}"), 16 * b.half + 16)
                        dve.wait_ge(sem(f"routed_in{b.par}"), 16 * T * b.half + 16 * T)
                        own.did(v.tensor_tensor(part[:], x3[b.par][:], routed[b.par][:], ALU.add))
                        own.wait()
                        dve.wait_ge(sem("y_ps"), b.b + 1)
                        v.tensor_tensor(xr[:], y_ps[b.par % 2], part[:], ALU.add).then_inc(sem("y_read"), 1)
                        dve.wait_ge(sem("y_read"), b.b + 1)
                        need(dve, sem(f"out{b.par}"), 16 * b.half)
                        layer_norm(v, own, xr, y[b.par], st, mv, ve, sem("var_ready"), sem("rstd_ready"), rstd, b.b + 1,
                                   sem("out_ready"))

                loop(dve, step, own)


class Bag:
    pass


def program(nc, io, stages=5):
    g, keep = Bag(), Bag()
    g.io = io
    with ExitStack() as ctx:
        sems = {}

        def sem(name):
            if name not in sems:
                sems[name] = nc.alloc_semaphore(name=name)
            return sems[name]

        def stage(run, *args):
            run(nc, g, keep, *args)
            nc.clear_and_free_semaphores(list(sems.values()))
            nc.all_engine_barrier()
            sems.clear()

        def sb(name, shape, dt=F32):
            return ctx.enter_context(nc.sbuf_tensor(name, shape, dt))

        g.sem = sem
        keep.ident = sb("ident", [P, P])
        keep.tri = sb("tri", [P, P])
        keep.ones = sb("ones", [P, P])
        keep.minus_half = sb("minus_half", [P, T])
        keep.iota = sb("iota", [P, E])
        keep.run = sb("run", [P, E])
        keep.prob = sb("prob", [P, NB * T])
        keep.slots = sb("slots", [P, NB * T])
        keep.rows = sb("rows", [P, NB * T], U32)
        keep.bias = sb("bias", [P, H, DELTA, P])
        stage(attention_one)
        if stages >= 2:
            stage(experts, "b", "xs_d", "ys_d", "w1", "w2", "b1", "b2")
        if stages >= 3:
            stage(attention_two)
        if stages >= 4:
            stage(experts, "d", "zs_d", "us_d", "rgu", "rd")
        if stages >= 5:
            stage(finish)


_SCRATCH = {"line_d": ([H, DELTA * UPAD], F32), "bias_d": ([H, P, DELTA, P], F32), "x1_d": ([NB, P, T, W], F32), "xs_d": ([ROWS, W], F32),
            "ys_d": ([BLOCKS * P, W], F32), "x3_d": ([NB, P, T, W], F32), "zs_d": ([ROWS, W], F32),
            "us_d": ([BLOCKS * P, W], F32), "parts_d": ([2, 2, 3, P, N], BF16)}


def _layout(**a):
    import numpy as np

    f = np.float32
    x = a["L0_attn_x"].reshape(NB, P, T, W)
    out = {
        "x": x,
        "xT": x.transpose(0, 3, 2, 1),
        "wk": np.concatenate([a["L0_attn_k1"], a["L0_attn_k2"], a["L0_attn_k3"]]).T,
        "wv": a["L0_attn_value_weight"].transpose(1, 0, 2).reshape(W, HA),
        "wo": a["L0_attn_output_weight"].transpose(0, 2, 1).reshape(HA // P, P, W).transpose(1, 0, 2),
        "sines": np.stack([a[f"L0_attn_{k}"].reshape(H * SP_ // P, P) for k in ("a1", "a2", "b1", "b2", "c")]).transpose(2, 0, 1),
        "wr": a["L0_ffn_Wr"],
        "br": np.broadcast_to(a["L0_ffn_br"], (P, E)),
        "w1": a["L0_ffn_W1"].transpose(1, 0, 2),
        "b1": np.broadcast_to(a["L0_ffn_b1"], (P, E, FH)),
        "w2": a["L0_ffn_W2"].reshape(E, 2, P, W).transpose(2, 0, 1, 3),
        "b2": np.broadcast_to(a["L0_ffn_b2"], (P, E, W)),
        "wq": a["L1_attn_Wqkv"][0:W].reshape(H, HD, W).transpose(2, 1, 0).reshape(W, W),
        "wkk": a["L1_attn_Wqkv"][W:2 * W].reshape(H, HD, W).transpose(2, 1, 0).reshape(W, W),
        "wvv": a["L1_attn_Wqkv"][2 * W:].T,
        "wout": a["L1_attn_Wout"].T,
        "wpos": a["L1_attn_Wpos"].T,
        "coeffs": a["L1_attn_coeffs"].T,
        "gw": a["L1_ffn_gate_w"].T,
        "sgu": np.stack([a["L1_ffn_shared_gate"], a["L1_ffn_shared_up"]]).transpose(2, 0, 1),
        "sd": a["L1_ffn_shared_down"].reshape(W, 2, P).transpose(2, 1, 0),
        "rgu": np.stack([a["L1_ffn_r_gate"], a["L1_ffn_r_up"]]).transpose(3, 1, 0, 2),
        "rd": a["L1_ffn_r_down"].reshape(E, W, 2, P).transpose(3, 0, 2, 1),
    }
    n = np.linspace(0.0, 1.0, N, dtype=f).reshape(P, T).T.reshape(N)
    out["pos"] = np.broadcast_to(n, (P, N))
    rows = np.arange(H * SP_).reshape(-1, P)
    out["hmask"] = (rows.T[:, :, None] // SP_ == np.arange(H)).astype(f)
    out["ident"] = np.eye(P, dtype=f)
    out["tri"] = np.triu(np.ones((P, P), f), 1)
    out["iota"] = np.broadcast_to(np.arange(E, dtype=f), (P, E))
    out["run0"] = np.broadcast_to(np.arange(E, dtype=f) * REGION, (P, E))
    out["lane"] = np.arange(P, dtype=f).reshape(P, 1)
    out["turn"] = np.broadcast_to(np.arange(BLOCKS, dtype=f), (P, BLOCKS))
    lag = np.arange(RES)[None, :] - np.arange(TAPS)[:, None]
    out["ramp"] = np.where(lag >= 0, np.linspace(0.0, 1.0, RES, dtype=f)[np.clip(lag, 0, RES - 1)], 0).astype(f)
    dist = np.abs(T * (np.arange(UPAD)[None, :] - (P - 1)) + np.arange(DELTA)[:, None] - (T - 1))
    level = np.clip(np.round(dist.astype(f) / f(N - 1) * f(RES - 1)).astype(int), 0, RES - 1)
    out["onehot"] = (level.reshape(1, -1) == np.arange(RES)[:, None]).astype(f)
    return {k: np.ascontiguousarray(v) for k, v in out.items()}


def build(nc, arrays, stages=5):
    io = {}
    for name, a in arrays.items():
        io[name] = nc.dram_tensor(f"in_{name}", a.shape, mybir.dt.from_np(a.dtype), kind="ExternalInput").ap()
    for name, (shape, dt) in _SCRATCH.items():
        io[name] = nc.dram_tensor(name, shape, dt, kind="Internal").ap()
    io["out"] = nc.dram_tensor("out", [NB, P, T, W], F32, kind="ExternalOutput").ap()
    program(nc, io, stages)


def kernel(**inputs):
    import numpy as np
    import concourse.bacc as bacc
    from concourse.bass_utils import run_bass_kernel_spmd

    nc = bacc.Bacc("TRN2", target_bir_lowering=False, num_devices=1)
    arrays = _layout(**{k: np.asarray(v) for k, v in inputs.items()})
    build(nc, arrays)
    r = run_bass_kernel_spmd(nc, [{f"in_{k}": v for k, v in arrays.items()}], core_ids=[0])
    return r.results[0]["out"].reshape(NB, N, W)
```

```python
from contextlib import ExitStack

import concourse.bass as bass
from concourse import mybir

F32 = mybir.dt.float32
BF16 = mybir.dt.bfloat16
U32 = mybir.dt.uint32
I32 = mybir.dt.int32
ALU = mybir.AluOpType
ACT = mybir.ActivationFunctionType
AX = mybir.AxisListType.X

P = 128
NB, N, W = 16, 512, 128
T = N // P
H, A = 16, 64
HA = H * A
SP_ = 64
E = 8
FH = 256
TAPS, RES, NF = 101, 64, 4
HD = W // H
DELTA = 2 * T - 1
UPAD = 2 * P
GROUP = T * P
REGION = NB * N + GROUP
BLOCKS = NB * N // GROUP + E
SPARE = E * REGION
ROWS = SPARE + GROUP
EPS = 1e-5
TWO_PI = 6.283185307179586
ROUND = 12582912.0
LIMIT = 20.0
A_OWN = 72
C_OWN = 86
C_POOL = 12
E_OWN = 36


class Step:

    def __init__(self, b, half, par, mod=2):
        self.b, self.half, self.par, self.mod = b, half, par, mod

    def back(self, n=1):
        s = self
        for _ in range(n):
            s = Step(s.b - 1, s.half if s.par else s.half - 1, (s.par - 1) % s.mod, s.mod)
        return s

    def ahead(self):
        last = self.par == self.mod - 1
        return Step(self.b + 1, self.half + 1 if last else self.half, (self.par + 1) % self.mod, self.mod)


def at(b, mod=2):
    return Step(b, b // mod, b % mod, mod)


def steps(i, first, mod=2):
    return [Step(i * mod + (first + j), i + first // mod, j, mod) for j in range(mod)]


def need(eng, sem, n):
    if not (isinstance(n, int) and n <= 0):
        eng.wait_ge(sem, n)


def apart(eng, passed):
    eng.sem_inc(passed, 1)


class Own:

    def __init__(self, eng, sem, passed=None):
        self.eng, self.sem, self.passed = eng, sem, passed
        self.start, self.n, self.i, self.per = 0, 0, None, 0

    def did(self, ins):
        ins.then_inc(self.sem, 1)
        self.n += 1

    def wait(self, alone=False):
        done = self.start + self.n
        if self.i is not None:
            done = self.i * self.per + done
        need(self.eng, self.sem, done)
        if alone:
            apart(self.eng, self.passed)

    def enter(self, i, per):
        self.start, self.n, self.i, self.per = self.start + self.n, 0, i, per

    def leave(self, trips):
        assert self.n == self.per, f"signals of a pass: {self.n}, not {self.per}"
        self.start, self.n, self.i = self.start + self.per * trips, 0, None


def norm_stats(v, own, src, st, mv, ve, var_ready):
    for t in range(T):
        own.did(v.bn_stats(st[:, t, :], src[:, t, :]))
    own.wait(alone=True)
    for t in range(T):
        own.did(v.bn_aggr(mv[:, t, :], st[:, t, :]))
    own.wait()
    v.tensor_scalar(ve[:], mv[:, :, 1], EPS, None, ALU.add).then_inc(var_ready, 1)


def norm_apply(v, src, dst, mv, rstd_ready, rstd, n, done):
    v.wait_ge(rstd_ready, n)
    for t in range(T):
        ins = v.tensor_scalar(dst[:, t, :], src[:, t, :], mv[:, t, 0:1], rstd[:, t:t + 1], ALU.subtract, ALU.mult)
    ins.then_inc(done, 1)


def layer_norm(v, own, src, dst, st, mv, ve, var_ready, rstd_ready, rstd, n, done):
    norm_stats(v, own, src, st, mv, ve, var_ready)
    norm_apply(v, src, dst, mv, rstd_ready, rstd, n, done)


def route(v, own, k, lg, top, idx, idxf, oh):
    apart(own.eng, own.passed)
    for t in range(T):
        own.did(v.max(top[:, t, :], lg[:, t, :]))
    own.wait(alone=True)
    for t in range(T):
        own.did(v.max_index(idx[:, t, :], top[:, t, :], lg[:, t, :]))
    own.wait()
    own.did(v.tensor_copy(idxf[:], idx[:, :, 0]))
    own.wait()


def slots_of(v, own, k, runs, run, oh, before, total, sel, slotf):
    own.did(v.tensor_copy(runs[:, 0, :], run[:]))
    own.wait()
    for t in range(T):
        dst = runs[:, t + 1, :] if t < T - 1 else run[:]
        own.did(v.tensor_tensor(dst, total[:, t, :], runs[:, t, :], ALU.add))
        own.wait()
    own.did(v.tensor_tensor(sel[:], before, runs[:], ALU.add))
    own.wait()
    own.did(v.tensor_tensor(sel[:], sel[:], oh[:], ALU.mult))
    own.wait()
    own.did(v.tensor_reduce(slotf[:], sel[:], AX, ALU.add))
    own.wait()


def attention_one(nc, g, keep):
    io, sem = g.io, g.sem
    with ExitStack() as ctx:
        def sb(name, shape, dt=F32):
            return ctx.enter_context(nc.sbuf_tensor(name, shape, dt))

        bank = [ctx.enter_context(nc.psum_tensor(f"a_bank{i}", [P, 512], F32)) for i in range(8)]
        v_ps, t_ps, misc, y_ps = bank[0:4], bank[4:6], bank[6], bank[7]
        lg_ps = misc[:, 0:3 * T * H].rearrange("p (t k) -> p t k", t=T)
        cb_ps = misc[:, 0:H]
        rl_ps = misc[:, 0:T * E].rearrange("p (t e) -> p t e", t=T)
        before_ps = misc[:, 0:T * E].rearrange("p (t e) -> p t e", t=T)
        total_ps = misc[:, T * E:2 * T * E].rearrange("p (t e) -> p t e", t=T)

        wk = sb("wk", [P, 3 * H])
        wv = sb("wv", [P, HA])
        wo = sb("wo", [P, HA // P, W])
        wr = sb("wr", [P, E])
        br = sb("br", [P, E])
        xT = [sb(f"xT{i}", [P, T, P]) for i in range(2)]
        xtok = [sb(f"xtok{i}", [P, T, W]) for i in range(2)]
        p1 = sb("p1", [P, T, H])
        ep2 = sb("ep2", [P, T, H])
        z = sb("z", [P, T, 3 * H])
        ez = [sb(f"ez{i}", [P, T, 3 * H]) for i in range(2)]
        gt = sb("gt", [P, T, H])
        den = sb("den", [P, T, H])
        dg = [sb(f"dg{i}", [P, T, H]) for i in range(2)]
        qc = sb("qc", [P, T, H])
        sumc = sb("sumc", [P, T, H])
        r = [sb(f"r{i}", [P, T, H]) for i in range(2)]
        vp = [sb(f"vp{i}", [P, HA]) for i in range(2)]
        v2 = [sb(f"v2{i}", [P, HA]) for i in range(2)]
        q = sb("q", [P, T, HA])
        s1 = [sb(f"s1{i}", [P, T, HA]) for i in range(2)]
        base = sb("base", [P, HA])
        o = [sb(f"o{i}", [P, HA]) for i in range(2)]
        oT = [sb(f"oT{i}", [P, HA // P, P]) for i in range(2)]
        xr = sb("xr", [P, T, W])
        st = sb("st", [P, T, 6])
        mv = sb("mv", [P, T, 2])
        ve = sb("ve", [P, T])
        rstd = sb("rstd", [P, T])
        x1 = [sb(f"x1{i}", [P, T, W]) for i in range(2)]
        x1T = sb("x1T", [P, T, P])
        rl = sb("rl", [P, T, E])
        rsh = sb("rsh", [P, T, E])
        rex = sb("rex", [P, T, E])
        rsum = sb("rsum", [P, T])
        top = sb("top", [P, T, 8])
        idx = sb("idx", [P, T, 8], U32)
        idxf = sb("idxf", [P, T])
        oh = sb("oh", [P, T, E])
        runs = sb("runs", [P, T, E])
        sel = sb("sel", [P, T, E])
        slotf = sb("slotf", [P, T])
        slot = [sb(f"slot{i}", [P, T], U32) for i in range(2)]
        amp = sb("amp", [P, 5, H * SP_ // P])
        turns = sb("turns", [P, 4, H * SP_ // P])
        pos = sb("pos", [P, N])
        hmask = sb("hmask", [P, H * SP_ // P, H])
        cm = sb("cm", [P, H * SP_ // P, H])
        ph = [sb(f"ph{i}", [P, N]) for i in range(4)]
        rnd = [sb(f"rnd{i}", [P, N]) for i in range(2)]
        sine = [sb(f"sine{i}", [P, N]) for i in range(2)]
        coeffs = sb("coeffs", [TAPS, NF])
        ramp = sb("ramp", [TAPS, RES])
        wpos = sb("wpos", [NF, H])
        table = sb("table", [NF, RES])
        levels = sb("levels", [RES, H])
        onehot = sb("onehot", [RES, DELTA * UPAD])
        line = sb("line", [H, DELTA * UPAD])
        SB = H * SP_ // P
        C4 = DELTA * UPAD // 4

        def loop(eng, step, own=None, first=-1):
            def peeled(k):
                step(at(k), [0 <= k + 1 - n < NB for n in range(5)])

            for k in range(first, 3):
                peeled(k)
            with eng.Fori(0, NB // 2 - 2) as i:
                if own:
                    own.enter(i, A_OWN)
                for s in steps(i, 4):
                    step(s.back(), [True] * 5)
            if own:
                own.leave(NB // 2 - 2)
            for k in range(NB - 1, NB + 3):
                peeled(k)

        with nc.Block() as block:

            @block.sync
            def _(sp):
                for dst, src in ((amp, "sines"), (pos, "pos"), (hmask, "hmask")):
                    sp.dma_start(dst[:], io[src]).then_inc(sem("sines_in"), 16)
                for dst, src in ((wk, "wk"), (wv, "wv"), (keep.ident, "ident")):
                    sp.dma_start(dst[:], io[src]).then_inc(sem("wv_in"), 16)

                def load_turned(s):
                    need(sp, sem("v_ready"), 8 * (s.b - 1))
                    sp.dma_start(xT[s.par][:], io["xT"][bass.ds(s.b, 1)].rearrange("o w t p -> w (o t) p")
                                 ).then_inc(sem(f"xT_in{s.par}"), 16)

                def load(s):
                    need(sp, sem("y_read"), s.b - 1)
                    sp.dma_start(xtok[s.par][:], io["x"][bass.ds(s.b, 1)].rearrange("o p t w -> p (o t) w")
                                 ).then_inc(sem(f"xtok_in{s.par}"), 16)

                def store(s):
                    sp.wait_ge(sem("x1_ready"), s.b + 1)
                    sp.dma_start(io["x1_d"][bass.ds(s.b, 1)].rearrange("o p t w -> p (o t) w"), x1[s.par][:]
                                 ).then_inc(sem(f"x1_out{s.par}"), 16)

                load_turned(at(0))
                for dst, src in ((keep.tri, "tri"), (wo, "wo"), (wr, "wr"), (br, "br"), (keep.iota, "iota"),
                                 (keep.run, "run0"), (keep.turn, "turn")):
                    sp.dma_start(dst[:], io[src]).then_inc(sem("wo_in"), 16)
                for dst, src in ((coeffs, "coeffs"), (ramp, "ramp"), (wpos, "wpos"), (onehot, "onehot")):
                    sp.dma_start(dst[:], io[src]).then_inc(sem("bias_in"), 16)
                def make_bias():
                    sp.wait_ge(sem("line_ready"), 4)
                    sp.dma_start(io["line_d"], line[:]).then_inc(sem("line_out"), 16)
                    sp.wait_ge(sem("line_out"), 16)
                    for h in range(H):
                        src = bass.AP(io["line_d"].tensor, h * DELTA * UPAD + P - 1, [[UPAD, DELTA], [-1, P], [1, P]])
                        sp.dma_start(io["bias_d"][h].rearrange("p d q -> d p q"), src).then_inc(sem("bias_out"), 16)

                def step(s, on):
                    if on[0]:
                        load_turned(s.ahead())
                    if on[1]:
                        load(s)
                    if isinstance(s.b, int) and s.b == 0:
                        make_bias()
                    if isinstance(s.b, int) and s.b == 2:
                        sp.wait_ge(sem("bias_out"), 16 * H)
                        sp.dma_start(keep.bias[:], io["bias_d"].rearrange("h p d q -> p h d q")
                                     ).then_inc(sem("bias_ready"), 16)
                    if on[3]:
                        store(s.back(2))

                loop(sp, step, first=0)
                sp.wait_ge(sem("bias_ready"), 16)
                sp.wait_ge(sem("x1_out0"), 16 * NB // 2)
                sp.wait_ge(sem("x1_out1"), 16 * NB // 2)

            @block.tensor
            def _(pe):
                pe.wait_ge(sem("sines_in"), 48)
                for k in range(2 * SB):
                    pe.wait_ge(sem("sine_ready"), k + 1)
                    if k == 0:
                        pe.wait_ge(sem("cm_ready"), SB)
                    for t in range(T):
                        mm = nc.tensor.matmul(y_ps[:, (k // SB * T + t) * H:(k // SB * T + t + 1) * H],
                                              sine[k % 2][:, t * P:(t + 1) * P], cm[:, k % SB, :],
                                              start=(k == 0 and t == 0), stop=(k % SB == SB - 1),
                                              skip_group_check=True)
                    mm.then_inc(sem("pos_sum"), 1)
                pe.wait_ge(sem("bias_in"), 64)
                nc.tensor.matmul(t_ps[0][0:NF, 0:RES], coeffs[:], ramp[:], start=True, stop=True).then_inc(sem("table_ps"), 1)
                pe.wait_ge(sem("table_sb"), 1)
                nc.tensor.matmul(misc[0:RES, 0:H], table[:], wpos[:], start=True, stop=True).then_inc(sem("table_ps"), 1)
                pe.wait_ge(sem("table_sb"), 2)
                for c in range(4):
                    need(pe, sem("line_ready"), c - 1)
                    nc.tensor.matmul(t_ps[c % 2][0:H, 0:C4], levels[:], onehot[:, c * C4:(c + 1) * C4], start=True,
                                     stop=True).then_inc(sem("line_ps"), 1)
                pe.wait_ge(sem("line_ready"), 4)
                pe.wait_ge(sem("wv_in"), 48)

                def upto(n):
                    return min(n, NB) if isinstance(n, int) else n

                def front_logits(s):
                    pe.wait_ge(sem(f"xT_in{s.par}"), 16 * s.half + 16)
                    need(pe, sem("cbase_read"), s.b)
                    need(pe, sem("count_read"), s.b - 3)
                    for t in range(T):
                        mm = nc.tensor.matmul(lg_ps[:, t, :], xT[s.par][:, t, :], wk[:], start=True, stop=True)
                    mm.then_inc(sem("lg_ready"), 1)

                def front_values(s, t, h):
                    if t == 0 and h == 0:
                        pe.wait_ge(sem(f"xT_in{s.par}"), 16 * s.half + 16)
                    need(pe, sem("v2_ready"), 8 * s.b + 2 * t + h - 3)
                    nc.tensor.matmul(v_ps[2 * (t % 2) + h][:], xT[s.par][:, t, :], wv[:, 512 * h:512 * h + 512],
                                     start=True, stop=True).then_inc(sem("v_ready"), 1)

                def back_base(s, h):
                    pe.wait_ge(sem("q_ready"), 3 * s.b + 3)
                    need(pe, sem("turn_taken"), 8 * s.b)
                    nc.tensor.matmul(t_ps[h][:], keep.tri[:], q[:, T - 1, 512 * h:512 * h + 512],
                                     start=True, stop=True).then_inc(sem("base_ready"), 1)

                def weights_base(s):
                    pe.wait_ge(sem("sumc_ready"), s.b + 1)
                    need(pe, sem("rl_read"), upto(s.b - 2))
                    nc.tensor.matmul(cb_ps, keep.tri[:], qc[:, T - 1, :], start=True, stop=True
                                     ).then_inc(sem("cbase_ready"), 1)

                def back_turn(s, t):
                    pe.wait_ge(sem("o_ready"), 4 * s.b + t + 1)
                    for h in range(2):
                        if t == 0:
                            pe.wait_ge(sem("base_taken"), 2 * s.b + h + 1)
                        else:
                            pe.wait_ge(sem("turn_taken"), 8 * s.b + 2 * t + h - 1)
                        for k in range(4):
                            c = (4 * h + k) * P
                            mm = nc.tensor.transpose(t_ps[h][:, k * P:(k + 1) * P], o[t % 2][:, c:c + P], keep.ident[:])
                        mm.then_inc(sem("turn_ready"), 1)

                def back_out(s, t):
                    if t == 0:
                        need(pe, sem("y_read"), s.b)
                    pe.wait_ge(sem("turn_taken"), 8 * s.b + 2 * t + 2)
                    for k in range(HA // P):
                        mm = nc.tensor.matmul(y_ps[:, t * W:(t + 1) * W], oT[t % 2][:, k, :], wo[:, k, :],
                                              start=(k == 0), stop=(k == HA // P - 1))
                    mm.then_inc(sem("y_ready"), 1)

                def route_turn(s):
                    pe.wait_ge(sem("x1_ready"), s.b + 1)
                    pe.wait_ge(sem("lg_read"), upto(s.b + 4))
                    need(pe, sem("count_read"), s.b)
                    for t in range(T):
                        mm = nc.tensor.transpose(misc[:, t * P:(t + 1) * P], x1[s.par][:, t, :], keep.ident[:])
                    mm.then_inc(sem("x1T_ready"), 1)

                def route_logits(s):
                    pe.wait_ge(sem("x1T_taken"), s.b + 1)
                    for t in range(T):
                        mm = nc.tensor.matmul(rl_ps[:, t, :], x1T[:, t, :], wr[:], start=True, stop=True)
                    mm.then_inc(sem("rl_ready"), 1)

                def route_count(s):
                    pe.wait_ge(sem("oh_ready"), s.b + 1)
                    pe.wait_ge(sem("cbase_read"), upto(s.b + 4))
                    nc.tensor.matmul(before_ps, keep.tri[:], oh[:], start=True, stop=True)
                    nc.tensor.matmul(total_ps, keep.ones[:], oh[:], start=True, stop=True).then_inc(sem("count_ready"), 1)

                def step(s, on):
                    if on[1]:
                        front_values(s, 0, 1)
                        front_values(s, 1, 0)
                    if on[2]:
                        back_base(s.back(), 0)
                        back_base(s.back(), 1)
                    if on[1]:
                        front_values(s, 1, 1)
                    if on[3]:
                        back_out(s.back(2), 2)
                        back_out(s.back(2), 3)
                    if on[1]:
                        front_values(s, 2, 0)
                    if on[4]:
                        route_count(s.back(3))
                    if on[1]:
                        front_values(s, 2, 1)
                    if on[2]:
                        back_turn(s.back(), 0)
                    if on[1]:
                        front_values(s, 3, 0)
                        front_values(s, 3, 1)
                    if on[2]:
                        back_turn(s.back(), 1)
                    if on[0]:
                        front_logits(s.ahead())
                        front_values(s.ahead(), 0, 0)
                    if on[2]:
                        back_out(s.back(), 0)
                    if on[3]:
                        route_turn(s.back(2))
                    if on[2]:
                        back_out(s.back(), 1)
                    if on[3]:
                        route_logits(s.back(2))
                    if on[2]:
                        back_turn(s.back(), 2)
                        back_turn(s.back(), 3)
                    if on[0]:
                        weights_base(s.ahead())

                pe.wait_ge(sem("pos_read"), 2)
                pe.wait_ge(sem("wo_in"), 112)
                pe.wait_ge(sem("const_ready"), 2)
                loop(pe, step)

            @block.scalar
            def _(act):
                for k in range(2 * SB):
                    act.wait_ge(sem("frac_ready"), k + 1)
                    need(act, sem("pos_sum"), k - 1)
                    nc.scalar.activation(sine[k % 2][:], ph[k % 4][:], ACT.Sin, scale=TWO_PI * (1 - 2e-7)
                                         ).then_inc(sem("sine_ready"), 1)
                act.wait_ge(sem("pos_read"), 2)
                nc.scalar.activation(ep2[:], gt[:], ACT.Exp).then_inc(sem("ep2_ready"), 1)

                def back_base(s, h):
                    need(act, sem("o_ready"), 4 * s.b)
                    act.wait_ge(sem("base_ready"), 2 * s.b + h + 1)
                    nc.scalar.copy(base[:, 512 * h:512 * h + 512], t_ps[h][:]).then_inc(sem("base_taken"), 1)

                def front_exp(s):
                    act.wait_ge(sem("lg_read"), s.b + 1)
                    need(act, sem("vp_ready"), 8 * (s.b - 1))
                    nc.scalar.activation(ez[s.par][:], z[:], ACT.Exp).then_inc(sem("ez_ready"), 1)

                def front_own(s, t, half):
                    if t == 0:
                        act.wait_ge(sem("dg_ready"), s.b + 1)
                    need(act, sem("s1_ready"), 4 * s.b + t - 1)
                    act.wait_ge(sem("vp_ready"), 8 * s.b + 2 * t + half + 1)
                    for k in range(H // 2):
                        h = H // 2 * half + k
                        ins = nc.scalar.activation(v2[t % 2][:, h * A:(h + 1) * A], v_ps[2 * (t % 2) + half][:, k * A:(k + 1) * A],
                                                   ACT.Copy, scale=dg[s.par][:, t, h:h + 1])
                    ins.then_inc(sem("v2_ready"), 1)

                def back_turn(s, t):
                    need(act, sem("y_ready"), 4 * s.b + t - 1)
                    for h in range(2):
                        act.wait_ge(sem("turn_ready"), 8 * s.b + 2 * t + h + 1)
                        nc.scalar.copy(oT[t % 2][:, 4 * h:4 * h + 4, :], t_ps[h][:].rearrange("p (k n) -> p k n", k=4)
                                       ).then_inc(sem("turn_taken"), 1)

                def route_turn(s):
                    act.wait_ge(sem("x1T_ready"), s.b + 1)
                    need(act, sem("rl_ready"), s.b)
                    nc.scalar.copy(x1T[:], misc[:].rearrange("p (t n) -> p t n", t=T)).then_inc(sem("x1T_taken"), 1)

                def route_exp(s):
                    act.wait_ge(sem("rsh_ready"), s.b + 1)
                    nc.scalar.activation(rex[:], rsh[:], ACT.Exp).then_inc(sem("rex_ready"), 1)

                def step(s, on):
                    if on[1]:
                        front_own(s, 0, 0)
                    if on[2]:
                        back_base(s.back(), 0)
                        back_base(s.back(), 1)
                    if on[1]:
                        front_own(s, 0, 1)
                        front_own(s, 1, 0)
                        front_own(s, 1, 1)
                    if on[2]:
                        back_turn(s.back(), 0)
                    if on[4]:
                        route_exp(s.back(3))
                    if on[1]:
                        front_own(s, 2, 0)
                        front_own(s, 2, 1)
                    if on[2]:
                        back_turn(s.back(), 1)
                    if on[0]:
                        front_exp(s.ahead())
                    if on[3]:
                        route_turn(s.back(2))
                    if on[1]:
                        front_own(s, 3, 0)
                        front_own(s, 3, 1)
                    if on[2]:
                        back_turn(s.back(), 2)
                        back_turn(s.back(), 3)

                loop(act, step)

            @block.gpsimd
            def _(pool):
                nc.gpsimd.memset(keep.ones[:], 1.0).then_inc(sem("const_ready"), 1)
                nc.gpsimd.memset(keep.minus_half[:], -0.5).then_inc(sem("const_ready"), 1)
                for k in range(2 * SB):
                    pool.wait_ge(sem("rnd_ready"), k + 1)
                    nc.gpsimd.tensor_tensor(ph[k % 4][:], ph[k % 4][:], rnd[k % 2][:], ALU.subtract
                                            ).then_inc(sem("frac_ready"), 1)

                def front_sum(s, t):
                    pool.wait_ge(sem("vp_ready"), 8 * s.b + 2 * t + 2)
                    if t == T - 1:
                        need(pool, sem("base_ready"), 2 * s.b)
                    if t >= 2:
                        pool.wait_ge(sem("q_ready"), 3 * s.b + t - 1)
                    nc.gpsimd.tensor_tensor(q[:, t, :], q[:, t - 1, :], vp[t % 2][:], ALU.add
                                            ).then_inc(sem("q_ready"), 1)

                def front_both(s, t):
                    if t == 0:
                        pool.wait_ge(sem("vp_ready"), 8 * s.b + 2)
                    else:
                        pool.wait_ge(sem("q_ready"), 3 * s.b + t)
                    pool.wait_ge(sem("v2_ready"), 8 * s.b + 2 * t + 2)
                    need(pool, sem("o_ready"), 4 * (s.b - 1))
                    nc.gpsimd.tensor_tensor(s1[s.par][:, t, :], q[:, t, :], v2[t % 2][:], ALU.add
                                            ).then_inc(sem("s1_ready"), 1)

                def back_rstd(s):
                    pool.wait_ge(sem("var_ready"), s.b + 1)
                    nc.gpsimd.tensor_tensor(rstd[:], ve[:], keep.minus_half[:], ALU.pow).then_inc(sem("rstd_ready"), 1)

                def route_scatter(s):
                    pool.wait_ge(sem("slot_ready"), s.b + 1)
                    apart(pool, sem("pool_passed"))
                    for t in range(T):
                        pool.indirect_dma_start(
                            out=io["xs_d"], out_offset=bass.IndirectOffsetOnAxis(ap=slot[s.par][:, t:t + 1], axis=0),
                            in_=x1[s.par][:, t, :], in_offset=None).then_inc(sem(f"scat{s.par}"), 16)

                def step(s, on):
                    if on[1]:
                        front_both(s, 0)
                    if on[3]:
                        back_rstd(s.back(2))
                    if on[1]:
                        front_sum(s, 1)
                        front_both(s, 1)
                        front_sum(s, 2)
                        front_sum(s, 3)
                        front_both(s, 2)
                        front_both(s, 3)
                    if on[4]:
                        route_scatter(s.back(3))

                pool.wait_ge(sem("const_ready"), 2)
                loop(pool, step)
                pool.wait_ge(sem("scat0"), 16 * T * NB // 2)
                pool.wait_ge(sem("scat1"), 16 * T * NB // 2)

            @block.vector
            def _(dve):
                v = nc.vector
                own = Own(dve, sem("a_own"), sem("dve_passed"))
                dve.wait_ge(sem("sines_in"), 48)
                own.did(v.tensor_scalar(turns[:], amp[:, 0:4, :], 1.0 / TWO_PI, None, ALU.mult))
                for k in range(SB):
                    v.tensor_scalar(cm[:, k, :], hmask[:, k, :], amp[:, 4, k:k + 1], None, ALU.mult).then_inc(sem("cm_ready"), 1)
                for k in range(2 * SB):
                    which, blk, b = k // SB, k % SB, k % 4
                    own.wait()
                    need(dve, sem("sine_ready"), k - 3)
                    own.did(v.tensor_scalar(ph[b][:], pos[:], turns[:, which, blk:blk + 1],
                                            turns[:, 2 + which, blk:blk + 1], ALU.mult, ALU.add))
                    own.wait()
                    need(dve, sem("frac_ready"), k - 1)
                    v.tensor_scalar(rnd[k % 2][:], ph[b][:], ROUND, ROUND, ALU.add, ALU.subtract).then_inc(sem("rnd_ready"), 1)
                dve.wait_ge(sem("pos_sum"), 2 * SB)
                v.tensor_copy(p1[:].rearrange("p t h -> p (t h)"), y_ps[:, 0:T * H]).then_inc(sem("pos_read"), 1)
                v.tensor_scalar(gt[:].rearrange("p t h -> p (t h)"), y_ps[:, T * H:2 * T * H], -LIMIT, LIMIT, ALU.max, ALU.min
                                ).then_inc(sem("pos_read"), 1)
                dve.wait_ge(sem("table_ps"), 1)
                v.tensor_copy(table[:], t_ps[0][0:NF, 0:RES]).then_inc(sem("table_sb"), 1)
                dve.wait_ge(sem("table_ps"), 2)
                v.tensor_copy(levels[:], misc[0:RES, 0:H]).then_inc(sem("table_sb"), 1)
                for c in range(4):
                    dve.wait_ge(sem("line_ps"), c + 1)
                    v.tensor_scalar(line[:, c * C4:(c + 1) * C4], t_ps[c % 2][0:H, 0:C4], -1.0, None, ALU.mult).then_inc(sem("line_ready"), 1)
                dve.wait_ge(sem("ep2_ready"), 1)
                dve.wait_ge(sem("wo_in"), 112)

                def heads(x):
                    return x.rearrange("p (h a) -> p h a", a=A)

                def back_den(s):
                    dve.wait_ge(sem("cbase_ready"), s.b + 1)
                    dve.wait_ge(sem("sumc_ready"), s.b + 1)
                    own.did(v.tensor_tensor(den[:], cb_ps.unsqueeze(1).to_broadcast([P, T, H]), sumc[:], ALU.add))
                    own.wait()
                    v.reciprocal(r[s.par][:], den[:]).then_inc(sem("cbase_read"), 1)

                def front_weights(s):
                    dve.wait_ge(sem("lg_ready"), s.b + 1)
                    need(dve, sem("ez_ready"), s.b)
                    own.did(v.tensor_tensor(z[:, :, 0:H], lg_ps[:, :, 0:H], p1[:], ALU.add))
                    own.did(v.tensor_scalar(z[:, :, H:3 * H], lg_ps[:, :, H:3 * H], -LIMIT, LIMIT, ALU.max, ALU.min))
                    own.wait()
                    v.tensor_scalar(z[:, :, 0:H], z[:, :, 0:H], -LIMIT, LIMIT, ALU.max, ALU.min).then_inc(sem("lg_read"), 1)

                def front_gains(s, k):
                    c = ez[s.par][:, :, 0:H]
                    if k == 0:
                        dve.wait_ge(sem("ez_ready"), s.b + 1)
                        own.did(v.tensor_tensor(gt[:], ez[s.par][:, :, 2 * H:3 * H], ep2[:], ALU.mult))
                        own.did(v.tensor_copy(qc[:, 0, :], c[:, 0]))
                    elif k == 1:
                        own.wait()
                        own.did(v.reciprocal(gt[:], gt[:]))
                        own.did(v.tensor_tensor(qc[:, 1, :], qc[:, 0, :], c[:, 1], ALU.add))
                    elif k == 2:
                        need(dve, sem("v2_ready"), 8 * (s.b - 1))
                        own.wait()
                        v.tensor_tensor(dg[s.par][:], gt[:], ez[s.par][:, :, H:2 * H], ALU.mult).then_inc(sem("dg_ready"), 1)
                        own.did(v.tensor_tensor(qc[:, 2, :], qc[:, 1, :], c[:, 2], ALU.add))
                    else:
                        own.wait()
                        own.did(v.tensor_tensor(qc[:, 3, :], qc[:, 2, :], c[:, 3], ALU.add))
                        own.wait()
                        dve.wait_ge(sem("dg_ready"), s.b + 1)
                        v.tensor_tensor(sumc[:], qc[:], dg[s.par][:], ALU.add).then_inc(sem("sumc_ready"), 1)

                def front_values(s, t, h):
                    if t == 0:
                        need(dve, sem("s1_ready"), 4 * s.b - 2)
                    else:
                        need(dve, sem("q_ready"), 3 * s.b + (0, -1, 1)[t - 1])
                    dst = q[:, 0, :] if t == 0 else vp[t % 2][:]
                    dve.wait_ge(sem("v_ready"), 8 * s.b + 2 * t + h + 1)
                    c = ez[s.par][:, t, h * H // 2:(h + 1) * H // 2].unsqueeze(2).to_broadcast([P, H // 2, A])
                    v.tensor_tensor(heads(dst[:, 512 * h:512 * h + 512]), heads(v_ps[2 * (t % 2) + h][:]), c, ALU.mult
                                    ).then_inc(sem("vp_ready"), 1)

                def back_add(s, t):
                    dve.wait_ge(sem("s1_ready"), 4 * s.b + t + 1)
                    if t == 0:
                        dve.wait_ge(sem("base_taken"), 2 * s.b + 2)
                    need(dve, sem("turn_ready"), 8 * s.b + 2 * t - 2)
                    v.tensor_tensor(o[t % 2][:], base[:], s1[s.par][:, t, :], ALU.add).then_inc(sem("o_sum"), 1)

                def back_heads(s, t):
                    if t == 0:
                        dve.wait_ge(sem("cbase_read"), s.b + 1)
                    dve.wait_ge(sem("o_sum"), 4 * s.b + t + 1)
                    v.tensor_tensor(heads(o[t % 2][:]), heads(o[t % 2][:]), r[s.par][:, t, :].unsqueeze(2).to_broadcast([P, H, A]),
                                    ALU.mult).then_inc(sem("o_ready"), 1)

                def back_norm(s):
                    dve.wait_ge(sem("y_ready"), 4 * s.b + 4)
                    dve.wait_ge(sem(f"xtok_in{s.par}"), 16 * s.half + 16)
                    v.tensor_tensor(xr[:].rearrange("p t w -> p (t w)"), y_ps[:],
                                    xtok[s.par][:].rearrange("p t w -> p (t w)"), ALU.add).then_inc(sem("y_read"), 1)
                    dve.wait_ge(sem("y_read"), s.b + 1)
                    norm_stats(v, own, xr, st, mv, ve, sem("var_ready"))

                def back_apply(s):
                    need(dve, sem(f"x1_out{s.par}"), 16 * s.half)
                    need(dve, sem(f"scat{s.par}"), 16 * T * s.half)
                    norm_apply(v, xr, x1[s.par], mv, sem("rstd_ready"), rstd, s.b + 1, sem("x1_ready"))

                def route_choose(s):
                    dve.wait_ge(sem("rl_ready"), s.b + 1)
                    v.tensor_tensor(rl[:], rl_ps, br[:].unsqueeze(1).to_broadcast([P, T, E]), ALU.add).then_inc(sem("rl_read"), 1)
                    dve.wait_ge(sem("rl_read"), s.b + 1)
                    route(v, own, keep, rl, top, idx, idxf, oh)
                    need(dve, sem("rex_ready"), s.b)
                    v.tensor_tensor(rsh[:], rl[:], top[:, :, 0:1].to_broadcast([P, T, E]), ALU.subtract).then_inc(sem("rsh_ready"), 1)
                    v.tensor_tensor(oh[:], keep.iota[:].unsqueeze(1).to_broadcast([P, T, E]),
                                    idxf[:].unsqueeze(2).to_broadcast([P, T, E]), ALU.is_equal).then_inc(sem("oh_ready"), 1)

                def route_slots(s):
                    dve.wait_ge(sem("rex_ready"), s.b + 1)
                    own.did(v.tensor_reduce(rsum[:], rex[:], AX, ALU.add))
                    dve.wait_ge(sem("count_ready"), s.b + 1)
                    dve.wait_ge(sem("oh_ready"), s.b + 1)
                    slots_of(v, own, keep, runs, keep.run, oh, before_ps, total_ps, sel, slotf)
                    v.reciprocal(keep.prob[:, bass.ds(T * s.b, T)], rsum[:]).then_inc(sem("count_read"), 1)
                    need(dve, sem(f"scat{s.par}"), 16 * T * s.half)
                    own.did(v.tensor_copy(keep.slots[:, bass.ds(T * s.b, T)], slotf[:]))
                    v.tensor_copy(slot[s.par][:], slotf[:]).then_inc(sem("slot_ready"), 1)

                def step(s, on):
                    if on[1]:
                        front_values(s, 0, 1)
                        front_values(s, 1, 0)
                        front_values(s, 1, 1)
                    if on[2]:
                        back_add(s.back(), 0)
                        back_add(s.back(), 1)
                        back_heads(s.back(), 0)
                    if on[3]:
                        back_norm(s.back(2))
                    if on[1]:
                        front_values(s, 2, 0)
                        front_values(s, 2, 1)
                    if on[2]:
                        back_heads(s.back(), 1)
                    if on[4]:
                        route_slots(s.back(3))
                    if on[1]:
                        front_values(s, 3, 0)
                    if on[3]:
                        back_apply(s.back(2))
                    if on[1]:
                        front_values(s, 3, 1)
                    if on[0]:
                        front_weights(s.ahead())
                    if on[2]:
                        back_add(s.back(), 2)
                    if on[0]:
                        front_gains(s.ahead(), 0)
                        front_gains(s.ahead(), 1)
                    if on[2]:
                        back_add(s.back(), 3)
                        back_heads(s.back(), 2)
                    if on[0]:
                        front_gains(s.ahead(), 2)
                    if on[2]:
                        back_heads(s.back(), 3)
                    if on[0]:
                        front_gains(s.ahead(), 3)
                    if on[3]:
                        route_choose(s.back(2))
                    if on[0]:
                        front_values(s.ahead(), 0, 0)
                        back_den(s.ahead())

                loop(dve, step, own)


def experts(nc, g, keep, tag, src, dst, weights, gated):
    io = g.io
    HIDDEN = (2 if gated else 1) * FH
    CHUNKS = FH // P
    OUT = HIDDEN if gated else HIDDEN + CHUNKS
    ALL = OUT + CHUNKS * W + (0 if gated else W)

    def sem(name):
        return g.sem(f"{tag}_{name}")

    with ExitStack() as ctx:
        def sb(name, shape, dt=F32):
            return ctx.enter_context(nc.sbuf_tensor(f"{tag}_{name}", shape, dt))

        bank = [ctx.enter_context(nc.psum_tensor(f"{tag}_bank{i}", [P, GROUP], F32)) for i in range(8)]
        turn_ps, gate_ps, h_ps = bank[0:2], bank[2:4], bank[4:6]
        y_ps = [b[:].rearrange("p (t w) -> p t w", t=T) for b in bank[6:8]]
        zeros = sb("zeros", [P, T, W])
        count = sb("count", [P, E])
        blocks = sb("blocks", [P, E])
        ones8 = sb("ones8", [P, E])
        ends = sb("ends", [P, E])
        offs = sb("offs", [P, E])
        first = sb("first", [P, E])
        fill = sb("fill", [P, E], I32)
        past = sb("past", [P, BLOCKS, E])
        ef = sb("ef", [P, BLOCKS])
        isf = sb("isf", [P, BLOCKS, E])
        rowf = sb("rowf", [P, BLOCKS])
        spare = sb("spare", [P, BLOCKS])
        row = sb("row", [P, BLOCKS], I32)
        expert = sb("expert", [P, BLOCKS], I32)
        chosen = sb("chosen", [P, NB * T])
        at_least = sb("at_least", [P, NB * T, E])
        its = sb("its", [P, NB * T, E])
        x = [sb(f"x{i}", [P, T, W]) for i in range(4)]
        w = [sb(f"w{i}", [P, ALL]) for i in range(4)]
        xT = [sb(f"xT{i}", [P, GROUP]) for i in range(2)]
        gate = [sb(f"gate{i}", [P, GROUP]) for i in range(2)]
        h = [sb(f"h{i}", [P, CHUNKS, T, P]) for i in range(2)]
        y = [sb(f"y{i}", [P, T, W]) for i in range(4)]

        def loop(eng, step):
            for k in range(4):
                step(at(k, 4), [k >= n for n in range(5)])
            with eng.Fori(0, BLOCKS // 4 - 1) as i:
                for s in steps(i, 4, 4):
                    step(s, [True] * 5)
            for k in range(BLOCKS, BLOCKS + 4):
                step(at(k, 4), [k - n < BLOCKS for n in range(5)])

        def which(eng, table, n, top):
            return eng.value_load(table[0:1, bass.ds(n, 1)], min_val=0, max_val=top)

        def rows_of(name, first):
            return io[name][bass.ds(first, GROUP), :].rearrange("(p t) w -> p t w", t=T)

        def fill_behind(eng, experts):
            eng.wait_ge(sem("zeros_ready"), 1)
            eng.wait_ge(sem("fill_ready"), 1)
            for e in experts:
                r = which(eng, fill, e, SPARE - GROUP)
                eng.dma_start(rows_of(src, r), zeros[:]).then_inc(sem("fill_out"), 16)

        with nc.Block() as block:

            @block.sync
            def _(sp):
                fill_behind(sp, range(0, E, 2))
                sp.dma_start(rows_of(src, SPARE), zeros[:]).then_inc(sem("fill_out"), 16)
                sp.wait_ge(sem("plan_ready"), 1)

                def step(s, on):
                    if on[0]:
                        e = which(sp, expert, s.b, E - 1)
                        if isinstance(s.b, int) and s.b == 0:
                            sp.wait_ge(sem("plan_ready"), 2)
                        r = which(sp, row, s.b, SPARE)
                        if isinstance(s.b, int) and s.b == 0:
                            sp.wait_ge(sem("fill_out"), 16 * E + 16)
                        need(sp, sem("y_ps"), s.b - 3)
                        if not gated:
                            need(sp, sem("y_ready"), s.b - 3)
                        sp.dma_start(x[s.par][:], rows_of(src, r)).then_inc(sem(f"x_in{s.par}"), 16)
                        sp.dma_start(w[s.par][:], io[weights][bass.ds(e, 1)].rearrange("o p f -> p (o f)")
                                     ).then_inc(sem(f"w_in{s.par}"), 16)
                    if on[4]:
                        b = s.back(4)
                        sp.wait_ge(sem("y_ready"), b.b + 1)
                        sp.dma_start(rows_of(dst, GROUP * b.b), y[b.par][:]).then_inc(sem(f"y_out{b.par}"), 16)

                loop(sp, step)
                for k in range(4):
                    sp.wait_ge(sem(f"y_out{k}"), 16 * BLOCKS // 4)

            @block.gpsimd
            def _(pool):
                nc.gpsimd.memset(zeros[:], 0.0).then_inc(sem("zeros_ready"), 1)
                nc.gpsimd.memset(ones8[:], 1.0).then_inc(sem("ones8_ready"), 1)

            @block.vector
            def _(dve):
                v = nc.vector
                own = Own(dve, sem("own"), sem("dve_passed"))
                v.tensor_copy(fill[:], keep.run[:]).then_inc(sem("fill_ready"), 1)
                dve.wait_ge(sem("ones8_ready"), 1)
                own.did(v.tensor_scalar(offs[:], keep.iota[:], float(REGION), None, ALU.mult))
                own.did(v.tensor_scalar(first[:], keep.iota[:], float(REGION), None, ALU.mult))
                own.wait()
                own.did(v.tensor_tensor(count[:], keep.run[:], offs[:], ALU.subtract))
                own.wait()
                own.did(v.tensor_scalar(blocks[:], count[:], GROUP - 1.0, 1.0 / GROUP, ALU.add, ALU.mult))
                own.wait()
                own.did(v.tensor_scalar(blocks[:], blocks[:], 0.5 / GROUP - 0.5, None, ALU.add))
                own.wait()
                own.did(v.tensor_scalar(blocks[:], blocks[:], ROUND, ROUND, ALU.add, ALU.subtract))
                own.wait()
                own.did(v.tensor_tensor_scan(ends[:], ones8[:], blocks[:], 0.0, ALU.mult, ALU.add))
                own.wait()
                many = [P, BLOCKS, E]
                own.did(v.tensor_tensor(past[:], keep.turn[:].unsqueeze(2).to_broadcast(many),
                                        ends[:].unsqueeze(1).to_broadcast(many), ALU.is_ge))
                own.wait()
                own.did(v.tensor_reduce(ef[:], past[:], AX, ALU.add))
                own.did(v.tensor_tensor(count[:], ends[:], blocks[:], ALU.subtract))
                own.wait()
                v.tensor_scalar(expert[:], ef[:], E - 1.0, None, ALU.min).then_inc(sem("plan_ready"), 1)
                own.did(v.tensor_tensor(isf[:], keep.iota[:].unsqueeze(1).to_broadcast(many),
                                        ef[:].unsqueeze(2).to_broadcast(many), ALU.is_equal))
                own.did(v.scalar_tensor_tensor(offs[:], count[:], -float(GROUP), offs[:], ALU.mult, ALU.add))
                own.did(v.tensor_scalar(spare[:], ef[:], E - 0.5, None, ALU.is_ge))
                own.did(v.tensor_scalar(rowf[:], keep.turn[:], float(GROUP), None, ALU.mult))
                own.wait()
                own.did(v.tensor_scalar(spare[:], spare[:], float(SPARE), None, ALU.mult))
                own.did(v.tensor_tensor(past[:], offs[:].unsqueeze(1).to_broadcast(many),
                                        rowf[:].unsqueeze(2).to_broadcast(many), ALU.add))
                own.wait()
                own.did(v.tensor_tensor(past[:], past[:], isf[:], ALU.mult))
                own.wait()
                own.did(v.tensor_reduce(rowf[:], past[:], AX, ALU.add))
                own.wait()
                v.tensor_tensor(row[:], rowf[:], spare[:], ALU.add).then_inc(sem("plan_ready"), 1)
                dve.wait_ge(sem("plan_ready"), 2)
                pairs = [P, NB * T, E]
                slots = keep.slots[:].unsqueeze(2).to_broadcast(pairs)
                own.did(v.tensor_tensor(at_least[:], slots, first[:].unsqueeze(1).to_broadcast(pairs), ALU.is_ge))
                own.wait()
                own.did(v.tensor_reduce(chosen[:], at_least[:], AX, ALU.add))
                own.wait()
                own.did(v.tensor_scalar(chosen[:], chosen[:], -1.0, None, ALU.add))
                own.wait()
                own.did(v.tensor_tensor(its[:], chosen[:].unsqueeze(2).to_broadcast(pairs),
                                        keep.iota[:].unsqueeze(1).to_broadcast(pairs), ALU.is_equal))
                own.wait()
                own.did(v.tensor_tensor(its[:], its[:], offs[:].unsqueeze(1).to_broadcast(pairs), ALU.mult))
                own.wait()
                own.did(v.tensor_reduce(chosen[:], its[:], AX, ALU.add))
                own.wait()
                v.tensor_tensor(keep.rows[:], keep.slots[:], chosen[:], ALU.subtract)

                def step(s, on):
                    if on[1] and gated:
                        b = s.back()
                        for c in range(CHUNKS):
                            dve.wait_ge(sem("gate_ready"), CHUNKS * b.b + c + 1)
                            if c == 0:
                                need(dve, sem("y_ps"), b.b - 1)
                            v.tensor_tensor(h[b.par % 2][:, c].rearrange("p t n -> p (t n)"), h_ps[c][:], gate[c][:], ALU.mult
                                            ).then_inc(sem("h_ready"), 1)
                    if on[2]:
                        b = s.back(2)
                        dve.wait_ge(sem("y_ps"), b.b + 1)
                        need(dve, sem(f"y_out{b.par}"), 16 * b.half)
                        if gated:
                            v.tensor_copy(y[b.par][:], y_ps[b.par % 2]).then_inc(sem("y_ready"), 1)
                        else:
                            v.tensor_tensor(y[b.par][:], y_ps[b.par % 2], w[b.par][:, ALL - W:ALL].unsqueeze(1).to_broadcast([P, T, W]),
                                            ALU.add).then_inc(sem("y_ready"), 1)

                loop(dve, step)

            @block.scalar
            def _(act):
                fill_behind(act, range(1, E, 2))

                def step(s, on):
                    if on[0]:
                        act.wait_ge(sem("turn_ps"), s.b + 1)
                        need(act, sem("hidden_ps"), CHUNKS * (s.b - 1))
                        nc.scalar.copy(xT[s.par % 2][:], turn_ps[s.par % 2][:]).then_inc(sem("xT_ready"), 1)
                    if on[1]:
                        b = s.back()
                        for c in range(CHUNKS):
                            act.wait_ge(sem("hidden_ps"), CHUNKS * b.b + c + 1)
                            if gated:
                                need(act, sem("h_ready"), CHUNKS * b.b + c - 1)
                                nc.scalar.activation(gate[c][:], gate_ps[c][:], ACT.Silu).then_inc(sem("gate_ready"), 1)
                            else:
                                if c == 0:
                                    need(act, sem("y_ps"), b.b - 1)
                                nc.scalar.activation(h[b.par % 2][:, c].rearrange("p t n -> p (t n)"), h_ps[c][:], ACT.Relu,
                                                     bias=w[b.par][:, HIDDEN + c:HIDDEN + c + 1]).then_inc(sem("h_ready"), 1)

                loop(act, step)

            @block.tensor
            def _(pe):
                def hidden(b, c):
                    need(pe, sem("h_ready"), CHUNKS * b.b + c - 1)
                    for k, ps in enumerate((gate_ps, h_ps) if gated else (h_ps,)):
                        f = k * FH + c * P
                        mm = nc.tensor.matmul(ps[c][:], w[b.par][:, f:f + P], xT[b.par % 2][:], start=True, stop=True)
                    mm.then_inc(sem("hidden_ps"), 1)

                def step(s, on):
                    if on[0]:
                        pe.wait_ge(sem(f"x_in{s.par}"), 16 * s.half + 16)
                        need(pe, sem("xT_ready"), s.b - 1)
                        for t in range(T):
                            mm = nc.tensor.transpose(turn_ps[s.par % 2][:, t * P:(t + 1) * P], x[s.par][:, t, :], keep.ident[:])
                        mm.then_inc(sem("turn_ps"), 1)
                    if on[1]:
                        b = s.back()
                        pe.wait_ge(sem(f"w_in{b.par}"), 16 * b.half + 16)
                        pe.wait_ge(sem("xT_ready"), b.b + 1)
                        hidden(b, 0)
                    if on[2]:
                        b = s.back(2)
                        pe.wait_ge(sem("h_ready"), CHUNKS * b.b + CHUNKS)
                        need(pe, sem("y_ready"), b.b - 1)
                        for t in range(T):
                            for c in range(CHUNKS):
                                mm = nc.tensor.matmul(y_ps[b.par % 2][:, t, :], h[b.par % 2][:, c, t, :],
                                                      w[b.par][:, OUT + c * W:OUT + (c + 1) * W],
                                                      start=(c == 0), stop=(c == CHUNKS - 1))
                        mm.then_inc(sem("y_ps"), 1)
                    if on[1]:
                        hidden(s.back(), 1)

                loop(pe, step)


def attention_two(nc, g, keep):
    io = g.io
    G = 4
    GROUPS = H // G
    PARTS = 3
    ROWS_QK = PARTS * PARTS * HD
    STACK = 16 * 2 * PARTS
    VC = HD + 1
    ARRAY = 32
    SLOTS = G * T
    ROUND_SLOTS = SLOTS // 2
    ROUNDS = 2 * GROUPS
    ALL = GROUPS * SLOTS
    LEAD = 6
    DVE_LEAD = 5
    ACT_LEAD = 2
    BANKS = 4
    BUFS = 8
    DVE_TILES = (4, 5)

    def sem(name):
        return g.sem(f"c_{name}")

    with ExitStack() as ctx:
        def sb(name, shape, dt=F32):
            return ctx.enter_context(nc.sbuf_tensor(f"c_{name}", shape, dt))

        s_ps = [ctx.enter_context(nc.psum_tensor(f"c_s{i}", [P, N], F32)) for i in range(BANKS)]
        pT_ps = [ctx.enter_context(nc.psum_tensor(f"c_turned{i}", [P, T, P], F32)) for i in range(2)]
        o_ps = ctx.enter_context(nc.psum_tensor("c_o", [P, N], F32))
        misc = ctx.enter_context(nc.psum_tensor("c_misc", [P, N], F32))
        tiles = misc[:].rearrange("p (t w) -> p t w", t=T)
        rl_ps = misc[:, 0:T * E].rearrange("p (t e) -> p t e", t=T)
        before_ps = misc[:, 64:64 + T * E].rearrange("p (t e) -> p t e", t=T)
        total_ps = misc[:, 128:128 + T * E].rearrange("p (t e) -> p t e", t=T)

        wq, wk, wv, wout = (sb(n, [P, W]) for n in ("wq", "wkk", "wvv", "wout"))
        gw = sb("gw", [P, E])
        x1 = sb("x1", [P, T, W])
        yb = sb("yb", [P, T, W])
        rows = sb("rows", [P, T], U32)
        st = sb("st", [P, T, 6])
        mv = sb("mv", [P, T, 2])
        ve = sb("ve", [P, T])
        rstd = sb("rstd", [P, T])
        x2 = [sb(f"x2{i}", [P, T, W]) for i in range(2)]
        xT = sb("xT", [P, T, P])
        qk = sb("qk", [P, 2, N])
        parts = [sb(f"parts{w}", [P, PARTS, N], BF16) for w in range(2)]
        qst = [sb(f"qst{i}", [ROWS_QK, H, N], BF16) for i in range(2)]
        kst = [sb(f"kst{i}", [ROWS_QK, H, N], BF16) for i in range(2)]
        vst = [sb(f"vst{i}", [P, T, H * VC + ARRAY - VC]) for i in range(2)]
        sums = [sb(f"sums{i}", [P, N]) for i in range(BUFS)]
        low = [sb(f"low{i}", [P, 1]) for i in range(BUFS)]
        pT = [sb(f"pT{i}", [P, T, G, 2 * P]) for i in range(2)]
        oT = sb("oT", [P, N])
        rden = sb("rden", [P, T, G])
        att = sb("att", [P, T, H, HD])
        x3 = sb("x3", [P, T, W])
        xs = sb("xs", [P, T, W])
        lg = sb("lg", [P, T, E])
        top = sb("top", [P, T, 8])
        idx = sb("idx", [P, T, 8], U32)
        idxf = sb("idxf", [P, T])
        oh = sb("oh", [P, T, E])
        runs = sb("runs", [P, T, E])
        sel = sb("sel", [P, T, E])
        slotf = sb("slotf", [P, T])
        slot = sb("slot", [P, T], U32)
        sig = sb("sig", [P, T])
        score = sb("score", [P, T])

        def split(s, eng, engine, ops):
            for w in range(2):
                eng.wait_ge(sem("qk_taken"), 2 * s.b + w + 1)
                need(eng, sem("parts_out"), 16 * (2 * s.b + w - 1))
                for a in range(PARTS - 1):
                    apart(eng, sem("split_passed"))
                    ops.did(engine.tensor_copy(parts[w][:, a], qk[:, w]))
                    ops.wait()
                    dst = qk[:, w] if a == 0 else parts[w][:, 2]
                    ins = engine.tensor_tensor(dst, qk[:, w], parts[w][:, a], ALU.subtract)
                    if a == 0:
                        ops.did(ins)
                        ops.wait()
                    else:
                        ins.then_inc(sem("parts_ready"), 1)

        def tile(n):
            j, n = n // SLOTS, n % SLOTS
            r, n = n // ROUND_SLOTS, n % ROUND_SLOTS
            return G * j + n // 2, 2 * r + n % 2

        def copied(s, n):
            r, m = ROUNDS * s.b + n // ROUND_SLOTS, n % ROUND_SLOTS
            before = sum(d < m for d in DVE_TILES)
            if m in DVE_TILES:
                return "copied_dve", len(DVE_TILES) * r + before + 1
            return "copied_act", (ROUND_SLOTS - len(DVE_TILES)) * r + m - before + 1

        def copy(s, n, eng, engine):
            r, m = n // ROUND_SLOTS, n % ROUND_SLOTS
            eng.wait_ge(sem("turned"), ALL * s.b + n + 1)
            need(eng, sem("pv_done"), ROUNDS * s.b + r - 1)
            engine(pT[r % 2][:, :, m // 2, m % 2 * P:(m % 2 + 1) * P], pT_ps[m % 2][:]
                   ).then_inc(sem(copied(s, n)[0]), 1)

        def later(s, n, front=True):
            return (s, n) if n < ALL else (s.ahead(), n - ALL) if front else None

        def bodies(eng, body, own=None, per=0):
            body(at(0), tail=False)
            with eng.Fori(0, NB // 2 - 1) as i:
                if own:
                    own.enter(i, per)
                for s in steps(i, 2):
                    body(s.back())
            if own:
                own.leave(NB // 2 - 1)
            body(at(NB - 1), front=False)

        with nc.Block() as block:

            @block.sync
            def _(sp):
                for d, name in ((wq, "wq"), (wk, "wkk"), (wv, "wvv"), (wout, "wout"), (gw, "gw")):
                    sp.dma_start(d[:], io[name]).then_inc(sem("w_in"), 16)

                def load(s):
                    need(sp, sem("x2_ready"), s.b)
                    sp.dma_start(x1[:], io["x1_d"][bass.ds(s.b, 1)].rearrange("o p t w -> p (o t) w")
                                 ).then_inc(sem("x1_in"), 16)

                def stack(s):
                    for w in range(2):
                        sp.wait_ge(sem("parts_ready"), 2 * s.b + w + 1)
                        sp.dma_start(io["parts_d"][s.par, w].rearrange("a p n -> p a n"), parts[w][:]
                                     ).then_inc(sem("parts_out"), 16)
                    sp.wait_ge(sem("parts_out"), 32 * s.b + 32)
                    apart(sp, sem("sp_passed"))
                    need(sp, sem("s_ps"), ALL * (s.b - 1))
                    part = P * N
                    for st, w, strides in ((kst[s.par], 1, (0, part)), (qst[s.par], 0, (part, 0))):
                        for a in range(PARTS):
                            src = bass.AP(io["parts_d"].tensor, (2 * s.par + w) * PARTS * part + a * strides[0],
                                          [[strides[1], PARTS], [H * N, HD], [1, H * N]])
                            sp.dma_start(st[a * PARTS * HD:(a + 1) * PARTS * HD].rearrange("r h n -> r (h n)"), src
                                         ).then_inc(sem(f"stack_in{s.par}"), 16)

                def store(s):
                    sp.wait_ge(sem("x3_ready"), s.b + 1)
                    sp.dma_start(io["x3_d"][bass.ds(s.b, 1)].rearrange("o p t w -> p (o t) w"), x3[:]
                                 ).then_inc(sem("x3_out"), 16)

                def body(s, tail=True, front=True):
                    if front:
                        stack(s.ahead())
                        if not isinstance(s.b, int) or s.b + 2 < NB:
                            load(s.ahead().ahead())
                    if tail:
                        store(s.back())

                load(at(0))
                stack(at(0))
                load(at(1))
                body(at(0), tail=False)
                with sp.Fori(0, NB // 2 - 2) as i:
                    for s in steps(i, 2):
                        body(s.back())
                body(at(NB - 3))
                body(at(NB - 2))
                body(at(NB - 1), front=False)
                store(at(NB - 1))
                sp.wait_ge(sem("x3_out"), 16 * NB)

            @block.gpsimd
            def _(pool):
                def gather(s):
                    need(pool, sem("x2_ready"), s.b)
                    need(pool, sem("y_in"), 16 * T * s.b)
                    apart(pool, sem("pool_passed"))
                    nc.gpsimd.tensor_copy(rows[:], keep.rows[:, bass.ds(T * s.b, T)]).then_inc(sem("rows_ready"), 1)
                    pool.wait_ge(sem("rows_ready"), s.b + 1)
                    apart(pool, sem("pool_passed"))
                    for t in range(T):
                        pool.indirect_dma_start(
                            out=yb[:, t, :], out_offset=None, in_=io["ys_d"],
                            in_offset=bass.IndirectOffsetOnAxis(ap=rows[:, t:t + 1], axis=0)
                        ).then_inc(sem("y_in"), 16)

                def power(n):
                    pool.wait_ge(sem("var_ready"), n)
                    nc.gpsimd.tensor_tensor(rstd[:], ve[:], keep.minus_half[:], ALU.pow).then_inc(sem("rstd_ready"), 1)

                def scatter(s):
                    pool.wait_ge(sem("slot_ready"), s.b + 1)
                    apart(pool, sem("pool_passed"))
                    for t in range(T):
                        pool.indirect_dma_start(
                            out=io["zs_d"], out_offset=bass.IndirectOffsetOnAxis(ap=slot[:, t:t + 1], axis=0),
                            in_=xs[:, t, :], in_offset=None).then_inc(sem("scat"), 16)

                def body(s, tail=True, front=True):
                    if front:
                        power(2 * s.b + 1 if tail else 2)
                        split(s.ahead(), pool, nc.gpsimd, ops)
                    if tail:
                        power(2 * s.b + 2 if front else 2 * NB - 1)
                    if front and (not isinstance(s.b, int) or s.b + 2 < NB):
                        gather(s.ahead().ahead())
                    if tail:
                        scatter(s.back())

                ops = Own(pool, sem("pool_own"))
                gather(at(0))
                for k in range(2):
                    nc.gpsimd.memset(vst[k][:], 1.0).then_inc(sem("vst_ones"), 1)
                power(1)
                gather(at(1))
                body(at(0), tail=False)
                with pool.Fori(0, NB // 2 - 2) as i:
                    ops.enter(i, C_POOL)
                    for s in steps(i, 2):
                        body(s.back())
                ops.leave(NB // 2 - 2)
                body(at(NB - 3))
                body(at(NB - 2))
                body(at(NB - 1), front=False)
                power(2 * NB)
                scatter(at(NB - 1))
                pool.wait_ge(sem("scat"), 16 * T * NB)

            @block.tensor
            def _(pe):
                def scores(s, n):
                    k = ALL * s.b + n
                    if n == 0:
                        pe.wait_ge(sem(f"stack_in{s.par}"), STACK * s.half + STACK)
                    need(pe, sem("low_ready"), k - BANKS + 1)
                    h, t = tile(n)
                    nc.tensor.matmul(s_ps[n % BANKS][:], qst[s.par][:, h, t * P:(t + 1) * P], kst[s.par][:, h, :],
                                     start=True, stop=True).then_inc(sem("s_ps"), 1)

                def turn(s, n):
                    pe.wait_ge(sem("exp_done"), ALL * s.b + n + 1)
                    name, count = copied(s, n - 2) if n >= 2 else copied(s.back(), n - 2 + ALL)
                    need(pe, sem(name), count)
                    for c in range(T):
                        mm = nc.tensor.transpose(pT_ps[n % 2][:, c, :], sums[n % BUFS][:, c * P:(c + 1) * P], keep.ident[:])
                    mm.then_inc(sem("turned"), 1)

                def values(s, r, c):
                    n = ROUNDS * s.b + r
                    if c == 0:
                        pe.wait_ge(sem("copied_act"), (ROUND_SLOTS - len(DVE_TILES)) * (n + 1))
                        pe.wait_ge(sem("copied_dve"), len(DVE_TILES) * (n + 1))
                        if r % 2 == 0:
                            need(pe, sem("o_taken"), GROUPS * s.b + r // 2)
                    for i in range(G):
                        f = (G * (r // 2) + i) * VC
                        mm = nc.tensor.matmul(o_ps[ARRAY * i:ARRAY * (i + 1), r % 2 * 2 * P:(r % 2 + 1) * 2 * P],
                                              vst[s.par][:, c, f:f + ARRAY], pT[r % 2][:, c, i, :], start=(c == 0), stop=(c == T - 1))
                    if c == T - 1:
                        mm.then_inc(sem("pv_done"), 1)

                def out_turn(s, j):
                    pe.wait_ge(sem("o_taken"), GROUPS * s.b + j + 1)
                    for t in range(T):
                        mm = nc.tensor.transpose(tiles[:, t, :], oT[:, t * P:(t + 1) * P], keep.ident[:])
                    mm.then_inc(sem("on_ps"), 1)

                def front_turn(s):
                    pe.wait_ge(sem("x2_ready"), s.b + 1)
                    for t in range(T):
                        mm = nc.tensor.transpose(tiles[:, t, :], x2[s.par][:, t, :], keep.ident[:])
                    mm.then_inc(sem("x2T_ps"), 1)

                def front_qk(s, w):
                    pe.wait_ge(sem("x2T_ready"), s.b + 1)
                    if w == 1:
                        pe.wait_ge(sem("qk_taken"), 2 * s.b + 1)
                    nc.tensor.matmul(misc[:], (wq, wk)[w][:], xT[:].rearrange("p t n -> p (t n)"), start=True, stop=True
                                     ).then_inc(sem("qk_ps"), 1)

                def front_v(s):
                    pe.wait_ge(sem("qk_taken"), 2 * s.b + 2)
                    for t in range(T):
                        mm = nc.tensor.matmul(tiles[:, t, :], xT[:, t, :], wv[:], start=True, stop=True)
                    mm.then_inc(sem("v_ps"), 1)

                def tail_turn(s):
                    pe.wait_ge(sem("on_read"), GROUPS * s.b + GROUPS)
                    for t in range(T):
                        mm = nc.tensor.transpose(tiles[:, t, :], att[:, t].rearrange("p h d -> p (h d)"), keep.ident[:])
                    mm.then_inc(sem("attT_ps"), 1)

                def tail_out(s):
                    pe.wait_ge(sem("attT_ready"), s.b + 1)
                    for t in range(T):
                        mm = nc.tensor.matmul(tiles[:, t, :], xT[:, t, :], wout[:], start=True, stop=True)
                    mm.then_inc(sem("y_ps"), 1)

                def route_turn(s):
                    pe.wait_ge(sem("x3_ready"), s.b + 1)
                    for t in range(T):
                        mm = nc.tensor.transpose(tiles[:, t, :], x3[:, t, :], keep.ident[:])
                    mm.then_inc(sem("x3T_ps"), 1)

                def route_logits(s):
                    pe.wait_ge(sem("x3T_ready"), s.b + 1)
                    for t in range(T):
                        mm = nc.tensor.matmul(rl_ps[:, t, :], xT[:, t, :], gw[:], start=True, stop=True)
                    mm.then_inc(sem("rl_ps"), 1)

                def route_count(s):
                    pe.wait_ge(sem("oh_ready"), s.b + 1)
                    nc.tensor.matmul(before_ps, keep.tri[:], oh[:], start=True, stop=True)
                    nc.tensor.matmul(total_ps, keep.ones[:], oh[:], start=True, stop=True).then_inc(sem("count_ready"), 1)

                def others(s, j, n, tail, front):
                    if n == 8 and (j > 0 or tail):
                        if j == 1:
                            pe.wait_ge(sem("y_read"), s.b) if tail else pe.wait_ge(sem("v_taken"), s.b + 2)
                        elif j == 2 and tail:
                            pe.wait_ge(sem("count_read"), s.b)
                        else:
                            pe.wait_ge(sem("on_read"), GROUPS * s.b + j - 1)
                        out_turn(*((s, j - 1) if j else (s.back(), GROUPS - 1)))
                    if front and (j, n) == (0, 12):
                        pe.wait_ge(sem("on_read"), GROUPS * s.b) if tail else pe.wait_ge(sem("v_taken"), 1)
                        front_turn(s.ahead())
                    if front and j == 0 and n in (13, 15):
                        front_qk(s.ahead(), int(n == 15))
                    if front and (j, n) == (1, 0):
                        front_v(s.ahead())
                    if tail and (j, n) == (1, 3):
                        if front:
                            pe.wait_ge(sem("v_taken"), s.b + 2)
                        tail_turn(s.back())
                    if tail and (j, n) == (1, 5):
                        tail_out(s.back())
                    if tail and (j, n) == (1, 12):
                        pe.wait_ge(sem("on_read"), GROUPS * s.b + 1)
                        route_turn(s.back())
                    if tail and (j, n) == (2, 0):
                        route_logits(s.back())
                    if tail and (j, n) == (2, 5):
                        route_count(s.back())

                def body(s, tail=True, front=True):
                    for j in range(GROUPS):
                        for n in range(SLOTS):
                            k = SLOTS * j + n
                            if later(s, k + LEAD, front):
                                scores(*later(s, k + LEAD))
                            turn(s, k)
                            r, c = k // ROUND_SLOTS - 1, k % ROUND_SLOTS - 2
                            if 0 <= c < T and (r >= 0 or tail):
                                values(*((s, r) if r >= 0 else (s.back(), ROUNDS - 1)), c)
                            others(s, j, n, tail, front)

                pe.wait_ge(sem("w_in"), 80)
                front_turn(at(0))
                front_qk(at(0), 0)
                front_qk(at(0), 1)
                front_v(at(0))
                pe.wait_ge(sem("v_taken"), 1)
                for n in range(LEAD):
                    scores(at(0), n)
                bodies(pe, body)
                s = at(NB - 1)
                for c in range(T):
                    values(s, ROUNDS - 1, c)
                pe.wait_ge(sem("on_read"), GROUPS * NB - 1)
                out_turn(s, GROUPS - 1)
                tail_turn(s)
                tail_out(s)
                pe.wait_ge(sem("y_read"), NB)
                route_turn(s)
                route_logits(s)
                route_count(s)

            @block.scalar
            def _(act):
                def exps(s, n):
                    act.wait_ge(sem("low_ready"), ALL * s.b + n + 1)
                    b = n % BUFS
                    nc.scalar.activation(sums[b][:], sums[b][:], ACT.Exp, bias=low[b][:], scale=-1.0).then_inc(sem("exp_done"), 1)

                def out_copy(s, j):
                    act.wait_ge(sem("pv_done"), ROUNDS * s.b + 2 * j + 2)
                    need(act, sem("on_ps"), GROUPS * s.b + j)
                    nc.scalar.copy(oT[:], o_ps[:]).then_inc(sem("o_taken"), 1)

                def front_turn(s):
                    act.wait_ge(sem("x2T_ps"), s.b + 1)
                    need(act, sem("v_ps"), s.b)
                    need(act, sem("rl_ps"), s.b - 2)
                    nc.scalar.copy(xT[:], tiles).then_inc(sem("x2T_ready"), 1)

                def front_qk(s, w):
                    act.wait_ge(sem("qk_ps"), 2 * s.b + w + 1)
                    need(act, sem("parts_ready"), 2 * s.b + w - 1)
                    nc.scalar.activation(qk[:, w], misc[:], ACT.Copy, scale=-HD ** -0.5 if w == 0 else 1.0
                                         ).then_inc(sem("qk_taken"), 1)

                def front_v(s):
                    act.wait_ge(sem("v_ps"), s.b + 1)
                    need(act, sem("pv_done"), ROUNDS * (s.b - 1))
                    for t in range(T):
                        ins = nc.scalar.copy(vst[s.par][:, t, 0:H * VC].rearrange("p (h d) -> p h d", d=VC)[:, :, 0:HD],
                                             tiles[:, t, :].rearrange("p (h d) -> p h d", h=H))
                    ins.then_inc(sem("v_taken"), 1)

                def tail_turn(s):
                    act.wait_ge(sem("attT_ps"), s.b + 1)
                    act.wait_ge(sem("v_ps"), min(s.b + 3, NB) if isinstance(s.b, int) else s.b + 3)
                    nc.scalar.copy(xT[:], tiles).then_inc(sem("attT_ready"), 1)

                def route_turn(s):
                    act.wait_ge(sem("x3T_ps"), s.b + 1)
                    nc.scalar.copy(xT[:], tiles).then_inc(sem("x3T_ready"), 1)

                def route_exp(s):
                    act.wait_ge(sem("oh_ready"), s.b + 1)
                    need(act, sem("xs_ready"), s.b)
                    nc.scalar.activation(sig[:], top[:, :, 0], ACT.Exp, scale=-1.0).then_inc(sem("sig_ready"), 1)

                def others(s, j, n, tail, front):
                    if n == 6 and (j > 0 or tail):
                        out_copy(*((s, j - 1) if j else (s.back(), GROUPS - 1)))
                    if front and (j, n) == (0, 11):
                        front_turn(s.ahead())
                    if front and j == 0 and n in (13, 15):
                        front_qk(s.ahead(), int(n == 15))
                    if front and (j, n) == (1, 0):
                        front_v(s.ahead())
                    if tail and (j, n) == (1, 4):
                        tail_turn(s.back())
                    if tail and (j, n) == (1, 12):
                        route_turn(s.back())
                    if tail and (j, n) == (2, 4):
                        route_exp(s.back())

                def body(s, tail=True, front=True):
                    for j in range(GROUPS):
                        for n in range(SLOTS):
                            k = SLOTS * j + n
                            if later(s, k + ACT_LEAD, front):
                                exps(*later(s, k + ACT_LEAD))
                            if n % ROUND_SLOTS not in DVE_TILES:
                                copy(s, k, act, nc.scalar.copy)
                            others(s, j, n, tail, front)

                act.wait_ge(sem("vst_ones"), 2)
                front_turn(at(0))
                front_qk(at(0), 0)
                front_qk(at(0), 1)
                front_v(at(0))
                for n in range(ACT_LEAD):
                    exps(at(0), n)
                bodies(act, body)
                s = at(NB - 1)
                out_copy(s, GROUPS - 1)
                tail_turn(s)
                route_turn(s)
                route_exp(s)

            @block.vector
            def _(dve):
                v = nc.vector
                own = Own(dve, sem("own"), sem("dve_passed"))
                own.did(v.tensor_scalar(keep.run[:], keep.iota[:], float(REGION), None, ALU.mult))
                own.wait()

                def front_sum(s):
                    dve.wait_ge(sem("x1_in"), 16 * s.b + 16)
                    dve.wait_ge(sem("y_in"), 16 * T * s.b + 16 * T)
                    own.did(v.tensor_tensor(yb[:], yb[:], keep.prob[:, bass.ds(T * s.b, T)].unsqueeze(2)
                                            .to_broadcast([P, T, W]), ALU.mult))

                def front_stats(s):
                    own.wait()
                    own.did(v.tensor_tensor(yb[:], yb[:], x1[:], ALU.add))
                    own.wait()
                    norm_stats(v, own, yb, st, mv, ve, sem("var_ready"))

                def front_apply(s, n):
                    norm_apply(v, yb, x2[s.par], mv, sem("rstd_ready"), rstd, n, sem("x2_ready"))

                def biased(s, n):
                    k = ALL * s.b + n
                    need(dve, sem("turned"), k - BUFS + 1)
                    dve.wait_ge(sem("s_ps"), k + 1)
                    apart(dve, sem("dve_passed"))
                    h, t = tile(n)
                    bias = keep.bias[:, h, T - 1 - t:DELTA - t, :].rearrange("p t q -> p (t q)")
                    v.tensor_tensor_reduce(sums[n % BUFS][:], s_ps[n % BANKS][:], bias, 1.0, 3.0e38, ALU.add, ALU.min, low[n % BUFS][:]
                                           ).then_inc(sem("low_ready"), 1)

                def out_norm(s, j):
                    dve.wait_ge(sem("on_ps"), GROUPS * s.b + j + 1)
                    if j == 0:
                        need(dve, sem("attT_ps"), s.b)
                    heads = tiles.rearrange("p t (h c) -> p t h c", c=ARRAY)
                    own.did(v.reciprocal(rden[:], heads[:, :, :, HD]))
                    own.wait()
                    v.tensor_tensor(att[:, :, G * j:G * j + G, :], heads[:, :, :, 0:HD],
                                    rden[:].unsqueeze(3).to_broadcast([P, T, G, HD]), ALU.mult).then_inc(sem("on_read"), 1)

                def residual(s):
                    need(dve, sem("x3_out"), 16 * s.b)
                    need(dve, sem("xs_ready"), s.b)
                    own.did(v.tensor_copy(x3[:], x2[s.par][:]))

                def tail_stats(s):
                    dve.wait_ge(sem("y_ps"), s.b + 1)
                    own.wait()
                    v.tensor_tensor(x3[:], tiles, x3[:], ALU.add).then_inc(sem("y_read"), 1)
                    dve.wait_ge(sem("y_read"), s.b + 1)
                    norm_stats(v, own, x3, st, mv, ve, sem("var_ready"))

                def tail_apply(s, n):
                    norm_apply(v, x3, x3, mv, sem("rstd_ready"), rstd, n, sem("x3_ready"))

                def route_choose(s):
                    dve.wait_ge(sem("rl_ps"), s.b + 1)
                    own.did(v.tensor_copy(lg[:], rl_ps))
                    own.wait()
                    route(v, own, keep, lg, top, idx, idxf, oh)
                    v.tensor_tensor(oh[:], keep.iota[:].unsqueeze(1).to_broadcast([P, T, E]),
                                    idxf[:].unsqueeze(2).to_broadcast([P, T, E]), ALU.is_equal).then_inc(sem("oh_ready"), 1)

                def route_score(s):
                    dve.wait_ge(sem("sig_ready"), s.b + 1)
                    own.did(v.tensor_scalar(score[:], sig[:], 1.0, None, ALU.add))
                    own.wait()
                    own.did(v.reciprocal(score[:], score[:]))
                    own.wait()
                    need(dve, sem("scat"), 16 * T * s.b)
                    dve.wait_ge(sem("x3_ready"), s.b + 1)
                    for t in range(T):
                        ins = v.tensor_scalar(xs[:, t, :], x3[:, t, :], score[:, t:t + 1], None, ALU.mult)
                    ins.then_inc(sem("xs_ready"), 1)

                def route_slots(s):
                    dve.wait_ge(sem("count_ready"), s.b + 1)
                    dve.wait_ge(sem("oh_ready"), s.b + 1)
                    slots_of(v, own, keep, runs, keep.run, oh, before_ps, total_ps, sel, slotf)
                    v.tensor_copy(keep.slots[:, bass.ds(T * s.b, T)], slotf[:]).then_inc(sem("count_read"), 1)
                    v.tensor_copy(slot[:], slotf[:]).then_inc(sem("slot_ready"), 1)

                def others(s, j, n, tail, front):
                    if n == 11 and (j > 0 or tail):
                        out_norm(*((s, j - 1) if j else (s.back(), GROUPS - 1)))
                    m = 2 * s.b + 1 if tail else 2
                    if front and j == 0 and n == 2:
                        front_sum(s.ahead())
                    if front and j == 0 and n == 3:
                        front_stats(s.ahead())
                    if front and j == 0 and n == 7:
                        front_apply(s.ahead(), m)
                    if tail and j == 1 and n == 8:
                        tail_stats(s.back())
                    if tail and j == 1 and n == 10:
                        tail_apply(s.back(), m + 1 if front else 2 * NB - 1)
                    if tail and j == 2 and n == 2:
                        route_choose(s.back())
                    if tail and j == 2 and n == 5:
                        route_score(s.back())
                    if tail and j == 2 and n == 5:
                        route_slots(s.back())
                    if j == 3 and n == 2:
                        residual(s)

                def body(s, tail=True, front=True):
                    for j in range(GROUPS):
                        for n in range(SLOTS):
                            k = SLOTS * j + n
                            if later(s, k + DVE_LEAD, front):
                                biased(*later(s, k + DVE_LEAD))
                            if n % ROUND_SLOTS in DVE_TILES:
                                copy(s, k, dve, v.tensor_copy)
                            others(s, j, n, tail, front)

                front_sum(at(0))
                front_stats(at(0))
                front_apply(at(0), 1)
                split(at(0), dve, v, own)
                for n in range(DVE_LEAD):
                    biased(at(0), n)
                bodies(dve, body, own, C_OWN)
                s = at(NB - 1)
                out_norm(s, GROUPS - 1)
                tail_stats(s)
                tail_apply(s, 2 * NB)
                route_choose(s)
                route_score(s)
                route_slots(s)


def finish(nc, g, keep):
    io = g.io
    CHUNKS = FH // P

    def sem(name):
        return g.sem(f"e_{name}")

    with ExitStack() as ctx:
        def sb(name, shape, dt=F32):
            return ctx.enter_context(nc.sbuf_tensor(f"e_{name}", shape, dt))

        bank = [ctx.enter_context(nc.psum_tensor(f"e_bank{i}", [P, N], F32)) for i in range(8)]
        turn_ps, gate_ps, up_ps = bank[0:2], bank[2:4], bank[4:6]
        y_ps = [b[:].rearrange("p (t w) -> p t w", t=T) for b in bank[6:8]]
        sgu = sb("sgu", [P, 2, FH])
        sd = sb("sd", [P, CHUNKS, W])
        x3 = [sb(f"x3{i}", [P, T, W]) for i in range(4)]
        rows = [sb(f"rows{i}", [P, T], U32) for i in range(4)]
        routed = [sb(f"routed{i}", [P, T, W]) for i in range(4)]
        xT = [sb(f"xT{i}", [P, N]) for i in range(2)]
        gate = [sb(f"gate{i}", [P, N]) for i in range(2)]
        h = [sb(f"h{i}", [P, CHUNKS, T, P]) for i in range(2)]
        part = sb("part", [P, T, W])
        xr = sb("xr", [P, T, W])
        st = sb("st", [P, T, 6])
        mv = sb("mv", [P, T, 2])
        ve = sb("ve", [P, T])
        rstd = sb("rstd", [P, T])
        y = [sb(f"y{i}", [P, T, W]) for i in range(4)]

        def loop(eng, step, own=None):
            for k in range(4):
                step(at(k, 4), [k >= n for n in range(5)])
            with eng.Fori(0, NB // 4 - 1) as i:
                if own:
                    own.enter(i, E_OWN)
                for s in steps(i, 4, 4):
                    step(s, [True] * 5)
            if own:
                own.leave(NB // 4 - 1)
            for k in range(NB, NB + 4):
                step(at(k, 4), [k - n < NB for n in range(5)])

        with nc.Block() as block:

            @block.sync
            def _(sp):
                sp.dma_start(sgu[:], io["sgu"]).then_inc(sem("w_in"), 16)
                sp.dma_start(sd[:], io["sd"]).then_inc(sem("w_in"), 16)

                def step(s, on):
                    if on[0]:
                        need(sp, sem("y_read"), s.b - 3)
                        sp.dma_start(x3[s.par][:], io["x3_d"][bass.ds(s.b, 1)].rearrange("o p t w -> p (o t) w")
                                     ).then_inc(sem(f"x3_in{s.par}"), 16)
                    if on[4]:
                        b = s.back(4)
                        sp.wait_ge(sem("out_ready"), b.b + 1)
                        sp.dma_start(io["out"][bass.ds(b.b, 1)].rearrange("o p t w -> p (o t) w"), y[b.par][:]
                                     ).then_inc(sem(f"out{b.par}"), 16)

                loop(sp, step)
                for k in range(4):
                    sp.wait_ge(sem(f"out{k}"), 16 * NB // 4)

            @block.gpsimd
            def _(pool):
                def gather(s):
                    need(pool, sem("y_read"), s.b - 3)
                    need(pool, sem(f"routed_in{s.par}"), 16 * T * s.half)
                    apart(pool, sem("pool_passed"))
                    nc.gpsimd.tensor_copy(rows[s.par][:], keep.rows[:, bass.ds(T * s.b, T)]).then_inc(sem("rows_ready"), 1)
                    pool.wait_ge(sem("rows_ready"), s.b + 1)
                    apart(pool, sem("pool_passed"))
                    for t in range(T):
                        pool.indirect_dma_start(
                            out=routed[s.par][:, t, :], out_offset=None, in_=io["us_d"],
                            in_offset=bass.IndirectOffsetOnAxis(ap=rows[s.par][:, t:t + 1], axis=0)
                        ).then_inc(sem(f"routed_in{s.par}"), 16)

                def step(s, on):
                    if on[2]:
                        b = s.back(2)
                        pool.wait_ge(sem("var_ready"), b.b + 1)
                        nc.gpsimd.tensor_tensor(rstd[:], ve[:], keep.minus_half[:], ALU.pow).then_inc(sem("rstd_ready"), 1)
                    if on[0]:
                        gather(s)

                loop(pool, step)

            @block.tensor
            def _(pe):
                def hidden(b, c):
                    need(pe, sem("h_ready"), CHUNKS * b.b + c - 1)
                    for k, ps in enumerate((gate_ps, up_ps)):
                        mm = nc.tensor.matmul(ps[c][:], sgu[:, k, c * P:(c + 1) * P], xT[b.par % 2][:], start=True, stop=True)
                    mm.then_inc(sem("hidden_ps"), 1)

                def step(s, on):
                    if on[0]:
                        pe.wait_ge(sem(f"x3_in{s.par}"), 16 * s.half + 16)
                        need(pe, sem("xT_ready"), s.b - 1)
                        for t in range(T):
                            mm = nc.tensor.transpose(turn_ps[s.par % 2][:, t * P:(t + 1) * P], x3[s.par][:, t, :], keep.ident[:])
                        mm.then_inc(sem("turn_ps"), 1)
                    if on[1]:
                        b = s.back()
                        pe.wait_ge(sem("xT_ready"), b.b + 1)
                        hidden(b, 0)
                    if on[2]:
                        b = s.back(2)
                        pe.wait_ge(sem("h_ready"), CHUNKS * b.b + CHUNKS)
                        need(pe, sem("y_read"), b.b - 1)
                        for t in range(T):
                            for c in range(CHUNKS):
                                mm = nc.tensor.matmul(y_ps[b.par % 2][:, t, :], h[b.par % 2][:, c, t, :], sd[:, c, :],
                                                      start=(c == 0), stop=(c == CHUNKS - 1))
                        mm.then_inc(sem("y_ps"), 1)
                    if on[1]:
                        hidden(s.back(), 1)

                pe.wait_ge(sem("w_in"), 32)
                loop(pe, step)

            @block.scalar
            def _(act):
                def step(s, on):
                    if on[0]:
                        act.wait_ge(sem("turn_ps"), s.b + 1)
                        need(act, sem("hidden_ps"), CHUNKS * (s.b - 1))
                        nc.scalar.copy(xT[s.par % 2][:], turn_ps[s.par % 2][:]).then_inc(sem("xT_ready"), 1)
                    if on[1]:
                        b = s.back()
                        for c in range(CHUNKS):
                            act.wait_ge(sem("hidden_ps"), CHUNKS * b.b + c + 1)
                            need(act, sem("h_ready"), CHUNKS * b.b + c - 1)
                            nc.scalar.activation(gate[c][:], gate_ps[c][:], ACT.Silu).then_inc(sem("gate_ready"), 1)

                loop(act, step)

            @block.vector
            def _(dve):
                v = nc.vector
                own = Own(dve, sem("own"), sem("dve_passed"))

                def step(s, on):
                    if on[3]:
                        b = s.back(3)
                        need(dve, sem(f"out{b.par}"), 16 * b.half)
                        norm_apply(v, xr, y[b.par], mv, sem("rstd_ready"), rstd, b.b + 1, sem("out_ready"))
                    if on[1]:
                        b = s.back()
                        need(dve, sem("y_ps"), b.b - 1)
                        for c in range(CHUNKS):
                            dve.wait_ge(sem("gate_ready"), CHUNKS * b.b + c + 1)
                            v.tensor_tensor(h[b.par % 2][:, c].rearrange("p t n -> p (t n)"), up_ps[c][:], gate[c][:], ALU.mult
                                            ).then_inc(sem("h_ready"), 1)
                    if on[2]:
                        b = s.back(2)
                        dve.wait_ge(sem(f"x3_in{b.par}"), 16 * b.half + 16)
                        dve.wait_ge(sem(f"routed_in{b.par}"), 16 * T * b.half + 16 * T)
                        own.did(v.tensor_tensor(part[:], x3[b.par][:], routed[b.par][:], ALU.add))
                        own.wait()
                        dve.wait_ge(sem("y_ps"), b.b + 1)
                        v.tensor_tensor(xr[:], y_ps[b.par % 2], part[:], ALU.add).then_inc(sem("y_read"), 1)
                        dve.wait_ge(sem("y_read"), b.b + 1)
                        norm_stats(v, own, xr, st, mv, ve, sem("var_ready"))

                loop(dve, step, own)


class Bag:
    pass


def program(nc, io, stages=5):
    g, keep = Bag(), Bag()
    g.io = io
    with ExitStack() as ctx:
        sems = {}

        def sem(name):
            if name not in sems:
                sems[name] = nc.alloc_semaphore(name=name)
            return sems[name]

        def stage(run, *args):
            run(nc, g, keep, *args)
            nc.clear_and_free_semaphores(list(sems.values()))
            nc.all_engine_barrier()
            sems.clear()

        def sb(name, shape, dt=F32):
            return ctx.enter_context(nc.sbuf_tensor(name, shape, dt))

        g.sem = sem
        keep.ident = sb("ident", [P, P])
        keep.tri = sb("tri", [P, P])
        keep.ones = sb("ones", [P, P])
        keep.minus_half = sb("minus_half", [P, T])
        keep.iota = sb("iota", [P, E])
        keep.run = sb("run", [P, E])
        keep.turn = sb("turn", [P, BLOCKS])
        keep.prob = sb("prob", [P, NB * T])
        keep.slots = sb("slots", [P, NB * T])
        keep.rows = sb("rows", [P, NB * T], U32)
        keep.bias = sb("bias", [P, H, DELTA, P])
        stage(attention_one)
        if stages >= 2:
            stage(experts, "b", "xs_d", "ys_d", "wb", False)
        if stages >= 3:
            stage(attention_two)
        if stages >= 4:
            stage(experts, "d", "zs_d", "us_d", "wd", True)
        if stages >= 5:
            stage(finish)


_SCRATCH = {"line_d": ([H, DELTA * UPAD], F32), "bias_d": ([H, P, DELTA, P], F32), "x1_d": ([NB, P, T, W], F32), "xs_d": ([ROWS, W], F32),
            "ys_d": ([BLOCKS * GROUP, W], F32), "x3_d": ([NB, P, T, W], F32), "zs_d": ([ROWS, W], F32),
            "us_d": ([BLOCKS * GROUP, W], F32), "parts_d": ([2, 2, 3, P, N], BF16)}


def _layout(**a):
    import numpy as np

    f = np.float32
    x = a["L0_attn_x"].reshape(NB, P, T, W)
    out = {
        "x": x,
        "xT": x.transpose(0, 3, 2, 1),
        "wk": np.concatenate([a["L0_attn_k1"], a["L0_attn_k2"], a["L0_attn_k3"]]).T,
        "wv": a["L0_attn_value_weight"].transpose(1, 0, 2).reshape(W, HA),
        "wo": a["L0_attn_output_weight"].transpose(0, 2, 1).reshape(HA // P, P, W).transpose(1, 0, 2),
        "sines": np.stack([a[f"L0_attn_{k}"].reshape(H * SP_ // P, P) for k in ("a1", "a2", "b1", "b2", "c")]).transpose(2, 0, 1),
        "wr": a["L0_ffn_Wr"],
        "br": np.broadcast_to(a["L0_ffn_br"], (P, E)),
        "wb": np.concatenate([a["L0_ffn_W1"], a["L0_ffn_b1"].reshape(E, 2, P).transpose(0, 2, 1),
                              a["L0_ffn_W2"].reshape(E, 2, P, W).transpose(0, 2, 1, 3).reshape(E, P, 2 * W),
                              np.broadcast_to(a["L0_ffn_b2"][:, None, :], (E, P, W))], axis=2),
        "wq": a["L1_attn_Wqkv"][0:W].reshape(H, HD, W).transpose(2, 1, 0).reshape(W, W),
        "wkk": a["L1_attn_Wqkv"][W:2 * W].reshape(H, HD, W).transpose(2, 1, 0).reshape(W, W),
        "wvv": a["L1_attn_Wqkv"][2 * W:].T,
        "wout": a["L1_attn_Wout"].T,
        "wpos": a["L1_attn_Wpos"].T,
        "coeffs": a["L1_attn_coeffs"].T,
        "gw": a["L1_ffn_gate_w"].T,
        "sgu": np.stack([a["L1_ffn_shared_gate"], a["L1_ffn_shared_up"]]).transpose(2, 0, 1),
        "sd": a["L1_ffn_shared_down"].reshape(W, 2, P).transpose(2, 1, 0),
        "wd": np.concatenate([a["L1_ffn_r_gate"].transpose(0, 2, 1), a["L1_ffn_r_up"].transpose(0, 2, 1),
                              a["L1_ffn_r_down"].reshape(E, W, 2, P).transpose(0, 3, 2, 1).reshape(E, P, 2 * W)], axis=2),
    }
    n = np.linspace(0.0, 1.0, N, dtype=f).reshape(P, T).T.reshape(N)
    out["pos"] = np.broadcast_to(n, (P, N))
    rows = np.arange(H * SP_).reshape(-1, P)
    out["hmask"] = (rows.T[:, :, None] // SP_ == np.arange(H)).astype(f)
    out["ident"] = np.eye(P, dtype=f)
    out["tri"] = np.triu(np.ones((P, P), f), 1)
    out["iota"] = np.broadcast_to(np.arange(E, dtype=f), (P, E))
    out["run0"] = np.broadcast_to(np.arange(E, dtype=f) * REGION, (P, E))
    out["turn"] = np.broadcast_to(np.arange(BLOCKS, dtype=f), (P, BLOCKS))
    lag = np.arange(RES)[None, :] - np.arange(TAPS)[:, None]
    out["ramp"] = np.where(lag >= 0, np.linspace(0.0, 1.0, RES, dtype=f)[np.clip(lag, 0, RES - 1)], 0).astype(f)
    dist = np.abs(T * (np.arange(UPAD)[None, :] - (P - 1)) + np.arange(DELTA)[:, None] - (T - 1))
    level = np.clip(np.round(dist.astype(f) / f(N - 1) * f(RES - 1)).astype(int), 0, RES - 1)
    out["onehot"] = (level.reshape(1, -1) == np.arange(RES)[:, None]).astype(f)
    return {k: np.ascontiguousarray(v) for k, v in out.items()}


def build(nc, arrays, stages=5):
    io = {}
    for name, a in arrays.items():
        io[name] = nc.dram_tensor(f"in_{name}", a.shape, mybir.dt.from_np(a.dtype), kind="ExternalInput").ap()
    for name, (shape, dt) in _SCRATCH.items():
        io[name] = nc.dram_tensor(name, shape, dt, kind="Internal").ap()
    io["out"] = nc.dram_tensor("out", [NB, P, T, W], F32, kind="ExternalOutput").ap()
    program(nc, io, stages)


def kernel(**inputs):
    import numpy as np
    import concourse.bacc as bacc
    from concourse.bass_utils import run_bass_kernel_spmd

    nc = bacc.Bacc("TRN2", target_bir_lowering=False, num_devices=1)
    arrays = _layout(**{k: np.asarray(v) for k, v in inputs.items()})
    build(nc, arrays)
    r = run_bass_kernel_spmd(nc, [{f"in_{k}": v for k, v in arrays.items()}], core_ids=[0])
    return r.results[0]["out"].reshape(NB, N, W)
```
